# Optimizing a Trainium2 kernel written in Bass

```python
import numpy as np
import jax
import jax.numpy as jnp

def _softmax(x, axis=-1):
    return jax.nn.softmax(x, axis=axis)

def _gelu(x):
    return jax.nn.gelu(x, approximate=True)

def _silu(x):
    return jax.nn.silu(x)

def _sigmoid(x):
    return jax.nn.sigmoid(x)

def _layernorm(x, axis=-1, eps=1e-05):
    m = jnp.mean(x, axis=axis, keepdims=True)
    v = jnp.var(x, axis=axis, keepdims=True)
    return (x - m) / jnp.sqrt(v + eps)

def _scatter_add(tgt, idx, src, axis=0):
    return tgt.at[idx].add(src)

def _segment_sum(src, seg, n):
    return jax.ops.segment_sum(src, seg, n)
kernel_name = 'mk_adj_preln_d4_adj_r2_b6d3b1'

def setup_inputs(seed: int=0):
    np.random.seed(seed)
    _w = jnp.asarray

    def _rec_inputs():
        import jax
        import jax.numpy as jnp
        _gk = jax.random.key(seed)
        x = -0.0002928 + 1 * jax.random.normal(jax.random.fold_in(_gk, 1), (2048, 512), jnp.float32)
        _a = jax.random.bernoulli(jax.random.fold_in(_gk, 2), 0.00390625, (2048, 2048))
        _a = jnp.logical_or(_a, jnp.swapaxes(_a, -1, -2))
        _a = jnp.logical_or(_a, jnp.eye(2048, dtype=bool))
        _af = _a.astype(jnp.float32)
        adj = _af
        return (x, adj)
    x, adj = _rec_inputs()

    def _L0_gnn_setup():
        import jax, jax.numpy as jnp
        import numpy as np
        N = 2048
        D_IN = 512
        H = 16
        DH = D_IN // H
        ALPHA = 0.2
        MASK_VAL = -65500.0
        key = jax.random.key(seed)
        ks = jax.random.split(key, 7)
        x = jax.random.normal(ks[0], (N, D_IN), dtype=jnp.float32)
        adj = jax.random.randint(ks[1], (N, N), 0, 2).astype(jnp.float32)
        s = 1.0 / np.sqrt(D_IN)
        W_seq = jax.random.normal(ks[2], (D_IN, D_IN), dtype=jnp.float32) * s
        a1 = jax.random.normal(ks[3], (DH,), dtype=jnp.float32) / np.sqrt(DH)
        a2 = jax.random.normal(ks[4], (DH,), dtype=jnp.float32) / np.sqrt(DH)
        W_out = jax.random.normal(ks[5], (D_IN, D_IN), dtype=jnp.float32) * s
        b_out = jax.random.normal(ks[6], (D_IN,), dtype=jnp.float32) * 0.01
        return {'x': x, 'adj': adj, 'W_seq': W_seq, 'a1': a1, 'a2': a2, 'W_out': W_out, 'b_out': b_out}
    _L0_gnn_all = _L0_gnn_setup()
    _L0_gnn_in = {k: v for k, v in _L0_gnn_all.items() if k in ('W_seq', 'a1', 'a2', 'W_out', 'b_out')}
    del _L0_gnn_all

    def _L1_gnn_setup():
        import jax, jax.numpy as jnp
        import numpy as np
        D_IN, D_ATTN, STEPS = (512, 64, 2)
        P_TOP, TAU, LN_EPS = (0.9, 1.0, 1e-05)
        N = 2048

        def _xavier(key, shape):
            fan_in, fan_out = (shape[0], shape[1])
            lim = jnp.sqrt(6.0 / (fan_in + fan_out))
            return jax.random.uniform(key, shape, jnp.float32, -lim, lim)

        def _adj_from_feats(Xa, W1, W2, W3):
            Q = Xa @ W1
            K = Xa @ W3
            logits = Q @ W2 @ K.T / TAU
            n = logits.shape[1]
            order = jnp.argsort(-logits, axis=1)
            vals = jnp.take_along_axis(logits, order, axis=1)
            probs = jax.nn.softmax(vals, axis=1)
            csum = jnp.cumsum(probs, axis=1)
            k_i = jnp.sum(csum < P_TOP, axis=1) + 1
            keep = jnp.arange(n)[None, :] < k_i[:, None]
            masked_sorted = jnp.where(keep, vals, -jnp.inf)
            rows = jnp.arange(n)[:, None]
            masked = jnp.full_like(logits, -jnp.inf).at[rows, order].set(masked_sorted)
            return jax.nn.softmax(masked, axis=1)
        key = jax.random.key(seed)
        ks = jax.random.split(key, 12)
        X = jax.random.normal(ks[0], (N, D_IN), jnp.float32)
        S = jax.random.uniform(ks[1], (N, N), jnp.float32)
        W1 = _xavier(ks[2], (D_IN, D_ATTN))
        W3 = _xavier(ks[3], (D_IN, D_ATTN))
        W2 = _xavier(ks[4], (D_ATTN, D_ATTN))
        U1_0 = _xavier(ks[5], (D_IN, D_IN))
        U1_1 = _xavier(ks[6], (D_IN, D_IN))
        U2_0 = _xavier(ks[7], (D_IN, D_IN))
        U2_1 = _xavier(ks[8], (D_IN, D_IN))
        gamma = jnp.ones((D_IN,), jnp.float32)
        beta = jnp.zeros((D_IN,), jnp.float32)
        return {'X': X, 'S': S, 'W1': W1, 'W2': W2, 'W3': W3, 'U1_0': U1_0, 'U1_1': U1_1, 'U2_0': U2_0, 'U2_1': U2_1, 'gamma': gamma, 'beta': beta}
    _L1_gnn_all = _L1_gnn_setup()
    _L1_gnn_in = {k: v for k, v in _L1_gnn_all.items() if k in ('W1', 'W2', 'W3', 'U1_0', 'U1_1', 'U2_0', 'U2_1', 'gamma', 'beta')}
    del _L1_gnn_all

    def _L2_gnn_setup():
        import jax, jax.numpy as jnp
        import numpy as np
        import math
        SENT_DIM = 512
        N_SENT = 2048
        key = jax.random.key(seed)
        ks = jax.random.split(key, 8)
        D = SENT_DIM
        s = 1.0 / math.sqrt(D)
        return {'sent_embed': jax.random.normal(ks[0], (N_SENT, D), dtype=jnp.float32), 'adj_tensor': jax.random.randint(ks[1], (N_SENT, N_SENT), 0, 2).astype(jnp.float32), 'W_q': jax.random.uniform(ks[2], (D, D), jnp.float32, -s, s), 'b_q': jax.random.uniform(ks[3], (D,), jnp.float32, -s, s), 'W_k': jax.random.uniform(ks[4], (D, D), jnp.float32, -s, s), 'b_k': jax.random.uniform(ks[5], (D,), jnp.float32, -s, s), 'W_v': jax.random.uniform(ks[6], (D, D), jnp.float32, -s, s), 'b_v': jax.random.uniform(ks[7], (D,), jnp.float32, -s, s)}
    _L2_gnn_all = _L2_gnn_setup()
    _L2_gnn_in = {k: v for k, v in _L2_gnn_all.items() if k in ('W_q', 'b_q', 'W_k', 'b_k', 'W_v', 'b_v')}
    del _L2_gnn_all

    def _L3_gnn_setup():
        import jax, jax.numpy as jnp
        import numpy as np
        ALPHA = 0.2
        NEG = -9000000000000000.0
        N, NFEAT, NHID, NHEADS = (2048, 512, 64, 8)
        EMB = NHID * NHEADS
        key = jax.random.key(seed)
        ks = jax.random.split(key, 16)
        x = jax.random.normal(ks[0], (N, NFEAT), dtype=jnp.float32)
        adj = (jax.random.uniform(ks[1], (N, N)) < 0.01).astype(jnp.float32)
        adj = jnp.maximum(adj, jnp.eye(N, dtype=jnp.float32))
        s = 0.05
        W = jax.random.normal(ks[2], (NHEADS, NFEAT, NHID), dtype=jnp.float32) * s
        a1 = jax.random.normal(ks[3], (NHEADS, NHID), dtype=jnp.float32) * s
        a2 = jax.random.normal(ks[4], (NHEADS, NHID), dtype=jnp.float32) * s
        W1 = jax.random.normal(ks[5], (EMB // 2, EMB), dtype=jnp.float32) * s
        b1 = jnp.zeros((EMB // 2,), dtype=jnp.float32)
        W2 = jax.random.normal(ks[6], (NFEAT // 4, EMB // 2), dtype=jnp.float32) * s
        b2 = jnp.zeros((NFEAT // 4,), dtype=jnp.float32)
        W3 = jax.random.normal(ks[7], (NFEAT // 2, NFEAT // 4), dtype=jnp.float32) * s
        b3 = jnp.zeros((NFEAT // 2,), dtype=jnp.float32)
        W4 = jax.random.normal(ks[8], (NFEAT, NFEAT // 2), dtype=jnp.float32) * s
        b4 = jnp.zeros((NFEAT,), dtype=jnp.float32)
        return {'x': x, 'adj': adj, 'W': W, 'a1': a1, 'a2': a2, 'W1': W1, 'b1': b1, 'W2': W2, 'b2': b2, 'W3': W3, 'b3': b3, 'W4': W4, 'b4': b4}
    _L3_gnn_all = _L3_gnn_setup()
    _L3_gnn_in = {k: v for k, v in _L3_gnn_all.items() if k in ('W', 'a1', 'a2', 'W1', 'b1', 'W2', 'b2', 'W3', 'b3', 'W4', 'b4')}
    del _L3_gnn_all
    return {'x': x, 'adj': adj, 'L0_gnn_W_seq': _L0_gnn_in['W_seq'], 'L0_gnn_a1': _L0_gnn_in['a1'], 'L0_gnn_a2': _L0_gnn_in['a2'], 'L0_gnn_W_out': _L0_gnn_in['W_out'], 'L0_gnn_b_out': _L0_gnn_in['b_out'], 'L1_gnn_W1': _L1_gnn_in['W1'], 'L1_gnn_W2': _L1_gnn_in['W2'], 'L1_gnn_W3': _L1_gnn_in['W3'], 'L1_gnn_U1_0': _L1_gnn_in['U1_0'], 'L1_gnn_U1_1': _L1_gnn_in['U1_1'], 'L1_gnn_U2_0': _L1_gnn_in['U2_0'], 'L1_gnn_U2_1': _L1_gnn_in['U2_1'], 'L1_gnn_gamma': _L1_gnn_in['gamma'], 'L1_gnn_beta': _L1_gnn_in['beta'], 'L2_gnn_W_q': _L2_gnn_in['W_q'], 'L2_gnn_b_q': _L2_gnn_in['b_q'], 'L2_gnn_W_k': _L2_gnn_in['W_k'], 'L2_gnn_b_k': _L2_gnn_in['b_k'], 'L2_gnn_W_v': _L2_gnn_in['W_v'], 'L2_gnn_b_v': _L2_gnn_in['b_v'], 'L3_gnn_W': _L3_gnn_in['W'], 'L3_gnn_a1': _L3_gnn_in['a1'], 'L3_gnn_a2': _L3_gnn_in['a2'], 'L3_gnn_W1': _L3_gnn_in['W1'], 'L3_gnn_b1': _L3_gnn_in['b1'], 'L3_gnn_W2': _L3_gnn_in['W2'], 'L3_gnn_b2': _L3_gnn_in['b2'], 'L3_gnn_W3': _L3_gnn_in['W3'], 'L3_gnn_b3': _L3_gnn_in['b3'], 'L3_gnn_W4': _L3_gnn_in['W4'], 'L3_gnn_b4': _L3_gnn_in['b4']}

def reference(x, adj, L0_gnn_W_seq, L0_gnn_a1, L0_gnn_a2, L0_gnn_W_out, L0_gnn_b_out, L1_gnn_W1, L1_gnn_W2, L1_gnn_W3, L1_gnn_U1_0, L1_gnn_U1_1, L1_gnn_U2_0, L1_gnn_U2_1, L1_gnn_gamma, L1_gnn_beta, L2_gnn_W_q, L2_gnn_b_q, L2_gnn_W_k, L2_gnn_b_k, L2_gnn_W_v, L2_gnn_b_v, L3_gnn_W, L3_gnn_a1, L3_gnn_a2, L3_gnn_W1, L3_gnn_b1, L3_gnn_W2, L3_gnn_b2, L3_gnn_W3, L3_gnn_b3, L3_gnn_W4, L3_gnn_b4):
    import jax
    import jax.numpy as jnp

    def _L0_gnn_ref(x, adj, W_seq, a1, a2, W_out, b_out):
        import jax, jax.numpy as jnp
        import numpy as np
        N = 2048
        D_IN = 512
        H = 16
        DH = D_IN // H
        ALPHA = 0.2
        MASK_VAL = -65500.0
        seq = (x @ W_seq).reshape(N, H, DH)
        score1 = jnp.einsum('nhd,d->hn', seq, a1)
        score2 = jnp.einsum('nhd,d->hn', seq, a2)
        scores = score1[:, :, None] + score2[:, None, :]
        scores = jax.nn.leaky_relu(scores, negative_slope=ALPHA)
        scores = scores + (1.0 - adj)[None, :, :] * MASK_VAL
        attn = jax.nn.softmax(scores, axis=-1)
        hidden = jnp.einsum('hij,jhd->ihd', attn, seq).reshape(N, D_IN)
        hidden = hidden @ W_out + b_out
        return jax.nn.elu(hidden)

    def _L1_gnn_ref(X, S, W1, W2, W3, U1_0, U1_1, U2_0, U2_1, gamma, beta):
        import jax, jax.numpy as jnp
        import numpy as np
        D_IN, D_ATTN, STEPS = (512, 64, 2)
        P_TOP, TAU, LN_EPS = (0.9, 1.0, 1e-05)
        N = 2048

        def _xavier(key, shape):
            fan_in, fan_out = (shape[0], shape[1])
            lim = jnp.sqrt(6.0 / (fan_in + fan_out))
            return jax.random.uniform(key, shape, jnp.float32, -lim, lim)

        def _adj_from_feats(Xa, W1, W2, W3):
            Q = Xa @ W1
            K = Xa @ W3
            logits = Q @ W2 @ K.T / TAU
            n = logits.shape[1]
            order = jnp.argsort(-logits, axis=1)
            vals = jnp.take_along_axis(logits, order, axis=1)
            probs = jax.nn.softmax(vals, axis=1)
            csum = jnp.cumsum(probs, axis=1)
            k_i = jnp.sum(csum < P_TOP, axis=1) + 1
            keep = jnp.arange(n)[None, :] < k_i[:, None]
            masked_sorted = jnp.where(keep, vals, -jnp.inf)
            rows = jnp.arange(n)[:, None]
            masked = jnp.full_like(logits, -jnp.inf).at[rows, order].set(masked_sorted)
            return jax.nn.softmax(masked, axis=1)
        n = X.shape[0]
        S = S + jnp.eye(n, dtype=X.dtype)
        R = S / jnp.clip(S.sum(axis=1, keepdims=True), 1e-12)
        Z = jnp.zeros_like(X)
        Xf, Xa = (X, X)
        U1s, U2s = ((U1_0, U1_1), (U2_0, U2_1))
        for s in range(STEPS):
            A = _adj_from_feats(Xa, W1, W2, W3)
            Xf = R @ Xf
            Xa = A @ Xa
            Z = Z + (Xf @ U1s[s] + Xa @ U2s[s])
        Y = X + Z
        mu = Y.mean(axis=-1, keepdims=True)
        var = Y.var(axis=-1, keepdims=True)
        return (Y - mu) * jax.lax.rsqrt(var + LN_EPS) * gamma + beta

    def _L2_gnn_ref(sent_embed, adj_tensor, W_q, b_q, W_k, b_k, W_v, b_v):
        import jax, jax.numpy as jnp
        import numpy as np
        import math
        SENT_DIM = 512
        N_SENT = 2048
        q = sent_embed @ W_q.T + b_q
        k = sent_embed @ W_k.T + b_k
        v = sent_embed @ W_v.T + b_v
        scale = 1.0 / math.sqrt(sent_embed.shape[-1])
        z = scale * (q @ k.T)
        spare_z = z * adj_tensor
        spare_z = jnp.where(spare_z == 0.0, jnp.asarray(-10000.0, spare_z.dtype), spare_z)
        attn = jax.nn.softmax(spare_z, axis=1)
        out = attn @ v
        return jax.nn.relu(out)

    def _L3_gnn_ref(x, adj, W, a1, a2, W1, b1, W2, b2, W3, b3, W4, b4):
        import jax, jax.numpy as jnp
        import numpy as np
        ALPHA = 0.2
        NEG = -9000000000000000.0
        N, NFEAT, NHID, NHEADS = (2048, 512, 64, 8)
        EMB = NHID * NHEADS
        Wh = jnp.einsum('nf,hfd->hnd', x, W)
        e_src = jnp.einsum('hnd,hd->hn', Wh, a1)
        e_dst = jnp.einsum('hnd,hd->hn', Wh, a2)
        e = jax.nn.leaky_relu(e_src[:, :, None] + e_dst[:, None, :], ALPHA)
        e = jnp.where(adj[None] > 0, e, NEG)
        att = jax.nn.softmax(e, axis=-1)
        h = jnp.einsum('hnm,hmd->hnd', att, Wh)
        h = jax.nn.elu(h)
        enc = jnp.transpose(h, (1, 0, 2)).reshape(x.shape[0], -1)
        out = jax.nn.relu(enc @ W1.T + b1)
        out = jax.nn.relu(out @ W2.T + b2)
        out = jax.nn.relu(out @ W3.T + b3)
        out = out @ W4.T + b4
        return out
    h = jnp.maximum(_layernorm(x, axis=-1), 0.0)
    x = x + _L0_gnn_ref(h, adj, L0_gnn_W_seq, L0_gnn_a1, L0_gnn_a2, L0_gnn_W_out, L0_gnn_b_out)
    h = jnp.maximum(_layernorm(x, axis=-1), 0.0)
    x = x + _L1_gnn_ref(h, adj, L1_gnn_W1, L1_gnn_W2, L1_gnn_W3, L1_gnn_U1_0, L1_gnn_U1_1, L1_gnn_U2_0, L1_gnn_U2_1, L1_gnn_gamma, L1_gnn_beta)
    h = jnp.maximum(_layernorm(x, axis=-1), 0.0)
    x = x + _L2_gnn_ref(h, adj, L2_gnn_W_q, L2_gnn_b_q, L2_gnn_W_k, L2_gnn_b_k, L2_gnn_W_v, L2_gnn_b_v)
    h = jnp.maximum(_layernorm(x, axis=-1), 0.0)
    x = x + _L3_gnn_ref(h, adj, L3_gnn_W, L3_gnn_a1, L3_gnn_a2, L3_gnn_W1, L3_gnn_b1, L3_gnn_W2, L3_gnn_b2, L3_gnn_W3, L3_gnn_b3, L3_gnn_W4, L3_gnn_b4)
    return x

_drawn_inputs = setup_inputs


def setup_inputs(seed=0):
    import zlib

    import numpy as np

    out = dict(_drawn_inputs(seed))
    spreads = {'L1_gnn_gamma': (1.0, 0.2),
     'L1_gnn_beta': (0.0, 0.1),
     'L3_gnn_b1': (0.0, 0.8),
     'L3_gnn_b2': (0.0, 0.674),
     'L3_gnn_b3': (0.0, 0.268),
     'L3_gnn_b4': (0.0, 0.1)}
    factors = {'L0_gnn_b_out': 3.574,
     'L2_gnn_W_q': 8.0,
     'L2_gnn_b_q': 31.228,
     'L2_gnn_W_k': 8.0,
     'L2_gnn_b_k': 64.0,
     'L2_gnn_b_v': 5.32,
     'L3_gnn_a1': 64.0,
     'L3_gnn_a2': 24.955}
    for name, (base, spread) in spreads.items():
        noise = np.random.default_rng([zlib.crc32(name.encode()), seed]).standard_normal(out[name].shape)
        drawn = base * np.exp(spread * noise) if base else spread * noise
        out[name] = jnp.asarray(drawn.astype(out[name].dtype))
    for name, factor in factors.items():
        out[name] = (out[name] * factor).astype(out[name].dtype)
    return out
```

```python
import concourse.bass as bass
from concourse import mybir
import math
from contextlib import ExitStack, contextmanager

F32 = mybir.dt.float32
BF16 = mybir.dt.bfloat16
ALU = mybir.AluOpType
ACT = mybir.ActivationFunctionType
AX = mybir.AxisListType
RMAX = bass.bass_isa.ReduceOp.max

P = 128
N = 2048
D = 512
T = N // P
KD = D // P
BANK = 512
LN_EPS = 1e-5
TOP_EXPONENT = 76.0
SLOPE = 0.2
TOP_P = 0.9
DEPTH = 9.94
HALVINGS = 16
V_COLS = 1408
S_COLS = N - V_COLS
NOTHING = -10000.0
W2N = 64


class Chain:

    def __init__(self, eng, sem, base=0):
        self.eng, self.sem, self.base, self.k = eng, sem, base, 0

    def __call__(self, ins):
        ins.then_inc(self.sem, 1)
        self.k += 1
        self.eng.wait_ge(self.sem, self.base + self.k)


class Core:

    WORDS = 53000

    def __init__(self, nc, ctx):
        self.nc, self.ctx = nc, ctx
        self.sb = ctx.enter_context(nc.sbuf_tensor("arena", [P, self.WORDS], F32))
        self.ps = ctx.enter_context(nc.psum_tensor("banks", [P, 8 * BANK], F32))
        self.at = 0

    def take(self, words, at=None):
        if at is not None:
            self.at = at
        a = self.at
        self.at += words
        assert self.at <= self.WORDS, self.at
        return self.sb[:, a:a + words]

    def bank(self, b, n=1):
        return self.ps[:, b * BANK:(b + n) * BANK]

    def sem(self, name):
        self.sems.append(self.stack.enter_context(self.nc.semaphore(name)))
        return self.sems[-1]

    @contextmanager
    def layer(self):
        self.sems = []
        with ExitStack() as self.stack:
            yield
            with self.nc.Block() as block:
                @block.sync
                def _(sp):
                    for s in self.sems:
                        sp.sem_clear(s)


def tile(ap, t):
    return ap[:, bass.ds(t, 1), :].rearrange("p a b -> p (a b)")


def rows(dram, t):
    return dram[bass.ds(t, 1), :, :].rearrange("a p b -> (a p) b")


def cols(ap, t, w):
    return ap[:, bass.ds(t * w, w)]


def layout(core):
    m = type("Buffers", (), {})()
    m.adj = core.take(T * N // 2, 0).bitcast(BF16).rearrange("p (t n) -> p t n", t=T)
    m.big_b = core.at
    core.take(T * D)
    m.big_c = core.at
    core.take(T * D)
    m.ring = core.at
    core.take(6 * N)
    m.w = core.at
    core.take(3456)
    m.small = core.at
    m.ident = core.take(P)
    m.rdeg = core.take(T)
    m.rstd = core.take(T)
    m.nmr = core.take(T)
    m.mv = core.take(2 * T).rearrange("p (t c) -> p t c", c=2)
    m.var = core.take(T)
    m.std = core.take(T)
    m.st = core.take(6)
    m.ag = core.take(2)
    m.ones = core.take(1).bitcast(BF16)
    m.zeros = core.take(BANK // 2).bitcast(BF16)
    m.bcol = core.take(16)
    m.free = core.at
    return m


def setup(core, m):
    nc = core.nc
    s = core.sem("identity_ready")
    with nc.Block() as block:
        @block.gpsimd
        def _(pool):
            nc.gpsimd.memset(m.ident[:, :], 0.0).then_inc(s, 1)
            nc.gpsimd.memset(m.ones[:, :], 1.0).then_inc(s, 1)
            nc.gpsimd.memset(m.zeros[:, :], 0.0).then_inc(s, 1)
            pool.wait_ge(s, 3)
            nc.gpsimd.affine_select(out=m.ident[:, :], in_=m.ident[:, :], compare_op=ALU.not_equal, fill=1.0,
                                    base=0, pattern=[[-1, P]], channel_multiplier=1).then_inc(s, 1)


def front(core, m, tag, x_dram, weights, loads=(), project=None, evac_dve=None, evac_act=None, banks=6,
          natural=None, prepare=None, pool_first=None, prepare_pe=None, act_own=False, dve_own=True):
    nc = core.nc
    sem = lambda n: core.sem(f"{tag}_{n}")
    X = core.take(T * D, m.ring).rearrange("p (t d) -> p t d", t=T)
    hs = core.take(2 * D).rearrange("p (u d) -> p u d", u=2)
    hT = core.take(2 * D).rearrange("p (u k n) -> p u k n", u=2, k=KD)
    x_in = [sem(f"x_loaded{c}") for c in range(4)]
    w_in = sem("weights_loaded")
    vecs, stats, root, norm = sem("vector_chain"), sem("variance_ready"), sem("root_ready"), sem("scales_ready")
    prep = sem("weights_prepared")
    h_ready, t_done, ht_ready = sem("h_ready"), sem("transposed"), sem("hT_ready")
    mm_done, dve_out, act_out, nat_out = sem("projected"), sem("vector_moved"), sem("scalar_moved"), sem("natural_moved")
    TC = T // 4

    with nc.Block() as block:
        @block.sync
        def _(sp):
            for c in range(4):
                sp.dma_start(X[:, c * TC:(c + 1) * TC, :],
                             x_dram[c * TC:(c + 1) * TC, :, :].rearrange("t p d -> p t d")).then_inc(x_in[c], 16)
            for dst, src in weights:
                sp.dma_start(dst, src).then_inc(w_in, 16)
            sp.wait_ge(w_in, 16 * len(weights))

        @block.vector
        def _(dve):
            own = Chain(dve, vecs)
            for c in range(4):
                dve.wait_ge(x_in[c], 16)
                for t in range(c * TC, (c + 1) * TC):
                    own(nc.vector.bn_stats(m.st[:, :], X[:, t]))
                    own(nc.vector.bn_aggr(m.mv[:, t], m.st[:, :]))
            nc.vector.tensor_scalar_add(m.var[:, :], m.mv[:, :, 1], LN_EPS).then_inc(stats, 1)
            if prepare is not None:
                dve.wait_ge(w_in, 16 * len(weights))
                prepare(nc, dve, own)
                dve.sem_inc(prep, 1)
            dve.wait_ge(root, 1)
            own(nc.vector.reciprocal(m.rstd[:, :], m.std[:, :]))
            nc.vector.scalar_tensor_tensor(m.nmr[:, :], m.mv[:, :, 0], -1.0, m.rstd[:, :],
                                           ALU.mult, ALU.mult).then_inc(norm, 1)
            dve.sem_inc(ht_ready, 2)
            if evac_dve is not None:
                dve.sem_inc(dve_out, 2)
            with dve.Fori(0, T // 2) as p:
                for u in range(2):
                    dve.wait_ge(t_done, p * 2 + (u + 1 + 2))
                    dve.wait_ge(mm_done, p * 2 + (u + 1))
                    nc.vector.tensor_copy(hT[:, u], core.bank(u).rearrange("p (k n) -> p k n", k=KD)) \
                        .then_inc(ht_ready, 1)
                if evac_dve is not None:
                    for u in range(2):
                        dve.wait_ge(mm_done, p * 2 + (u + 1 + 2))
                        evac_dve(nc, p * 2 + u, u).then_inc(dve_out, 1)

        @block.scalar
        def _(act):
            act.wait_ge(stats, 1)
            nc.scalar.activation(m.std[:, :], m.var[:, :], ACT.Sqrt).then_inc(root, 1)
            act.wait_ge(norm, 1)
            if evac_act is not None:
                act.sem_inc(act_out, 2)

            def normalise(t, u, ahead):
                act.wait_ge(t_done, ahead + 1)
                if natural is not None:
                    act.wait_ge(nat_out, ahead + 1)
                nc.scalar.activation(hs[:, u], tile(X, t), ACT.Relu, bias=cols(m.nmr, t, 1),
                                     scale=cols(m.rstd, t, 1)).then_inc(h_ready, 1)

            with act.Fori(0, T // 2) as p:
                for u in range(2):
                    normalise(p * 2 + u, u, p * 2 + u)
                if evac_act is not None:
                    for u in range(2):
                        act.wait_ge(mm_done, p * 2 + (u + 1 + 2))
                        evac_act(nc, p * 2 + u, u).then_inc(act_out, 1)

        @block.tensor
        def _(pe):
            pe.wait_ge(w_in, 16 * len(weights))
            if prepare is not None:
                pe.wait_ge(prep, 1)
            pe.sem_inc(t_done, 2)
            pe.sem_inc(mm_done, 2)
            with pe.Fori(0, T // 2) as p:
                for u in range(2):
                    pe.wait_ge(h_ready, p * 2 + (u + 1))
                    pe.wait_ge(ht_ready, p * 2 + (u + 1))
                    for k in range(KD):
                        last = nc.tensor.transpose(core.bank(u)[:, k * P:(k + 1) * P],
                                                   hs[:, u, k * P:(k + 1) * P], m.ident[:, :])
                    last.then_inc(t_done, 1)
                for u in range(2):
                    pe.wait_ge(ht_ready, p * 2 + (u + 1 + 2))
                    if evac_dve is not None:
                        pe.wait_ge(dve_out, p * 2 + (u + 1))
                    if evac_act is not None:
                        pe.wait_ge(act_out, p * 2 + (u + 1))
                    project(nc, hT[:, u], u).then_inc(mm_done, 1)

        @block.gpsimd
        def _(pool):
            if pool_first is not None:
                pool_first(nc, pool)
            if natural is not None:
                pool.sem_inc(nat_out, 2)
                with pool.Fori(0, T // 2) as p:
                    for u in range(2):
                        pool.wait_ge(h_ready, p * 2 + (u + 1))
                        nc.gpsimd.tensor_copy(tile(natural, p * 2 + u), hs[:, u]).then_inc(nat_out, 1)


def accumulate(nc, out, pairs):
    last = None
    for n, (lhsT, rhs) in enumerate(pairs):
        last = nc.tensor.matmul(out, lhsT, rhs, start=(n == 0), stop=(n == len(pairs) - 1))
    return last


def graph_attention(core, m, tag, heads, x_dram, adjT, w_dram, a1_dram, a2_dram, c_dram, degree):
    nc = core.nc
    H, DH = heads, D // heads
    m.adj_loads += 1
    W = core.take(KD * D, m.w).rearrange("p (k d) -> p k d", k=KD)
    a1, a2 = core.take(D), core.take(D)
    w12 = core.take(KD * 2 * H).rearrange("p (k h) -> p k h", k=KD)
    prod = core.take(KD * D, m.big_c).rearrange("p (k d) -> p k d", k=KD)
    V = core.take(T * D, m.big_c).rearrange("p (t d) -> p t d", t=T)
    hid = core.take(T * D, m.big_b).rearrange("p (t d) -> p t d", t=T)
    s_rows = core.take(2 * N, m.big_b).rearrange("p (s n) -> p s n", s=2)
    c_rows = core.take(N)
    S = core.take(T * 2 * H, m.free).rearrange("p (t h) -> p t h", t=T)
    G, FF = (core.take(T * H).rearrange("p (t h) -> p t h", t=T) for _ in range(2))
    top, colmax, rowtop = core.take(H), core.take(H), core.take(1)
    recip = core.take(T)

    def load_adjacency(nc, pool):
        for t in range(T):
            pool.dma_start(m.adj[:, t, :], adjT[t, :, :]).then_inc(m.adj_loaded, 16)

    def prepare(nc, dve, link):
        for n, a in enumerate((a1, a2)):
            link(nc.vector.tensor_tensor(prod[:, :, :], W[:, :, :], a.unsqueeze(1).broadcast_to([P, KD, D]), ALU.mult))
            for k in range(KD):
                link(nc.vector.tensor_reduce(w12[:, k, n * H:(n + 1) * H],
                                             prod[:, k].rearrange("p (h d) -> p h d", h=H), AX.X, ALU.add))

    def project(nc, hT, u):
        v, s = core.bank(2 + u), core.bank(4 + u)
        accumulate(nc, v[:, :], [(hT[:, k], W[:, k]) for k in range(KD)])
        accumulate(nc, s[:, 0:2 * H], [(hT[:, k], w12[:, k]) for k in range(KD)])
        accumulate(nc, s[0:H, P:2 * P], [(w12[:, k, 0:H], hT[:, k]) for k in range(KD)])
        return accumulate(nc, s[0:H, 2 * P:3 * P], [(w12[:, k, H:2 * H], hT[:, k]) for k in range(KD)])

    def evac_dve(nc, t, u):
        s = core.bank(4 + u)
        nc.vector.tensor_copy(s_rows[0:H, :, bass.ds(t * P, P)], s[0:H, P:3 * P].rearrange("p (s n) -> p s n", s=2))
        return nc.vector.tensor_copy(tile(S, t), s[:, 0:2 * H])

    def evac_act(nc, t, u):
        return nc.scalar.activation(tile(V, t), core.bank(2 + u), ACT.Copy)

    front(core, m, tag, x_dram, [(W[:, :, :], w_dram), (a1[:, :], a1_dram), (a2[:, :], a2_dram)],
          project=project, evac_dve=evac_dve, evac_act=evac_act, prepare=prepare, pool_first=load_adjacency)

    sem = lambda n: core.sem(f"{tag}_{n}")
    link_s, colmax_ready, top_ready, diff_ready = sem("v_chain"), sem("colmax_ready"), sem("top_ready"), sem("diff_ready")
    row_ready, c_ready, c_stored, exp_ready = sem("row_ready"), sem("c_ready"), sem("c_stored"), sem("exp_ready")
    with nc.Block() as block:
        @block.vector
        def _(dve):
            link = Chain(dve, link_s)
            link(nc.vector.tensor_reduce(colmax[:, :], S[:, :, H:2 * H].rearrange("p t h -> p h t"), AX.X, ALU.max))
            dve.sem_inc(colmax_ready, 1)
            link(nc.vector.tensor_reduce(rowtop[0:H, :], s_rows[0:H, 1, :], AX.X, ALU.max))
            link(nc.vector.tensor_scalar(c_rows[0:H, :], s_rows[0:H, 0, :], rowtop[0:H, 0:1], 1.0 - SLOPE,
                                         ALU.add, ALU.mult))
            nc.vector.tensor_scalar_min(c_rows[0:H, :], c_rows[0:H, :], TOP_EXPONENT).then_inc(row_ready, 1)
            dve.wait_ge(top_ready, 1)
            nc.vector.tensor_tensor(S[:, :, 0:H], S[:, :, H:2 * H], top.unsqueeze(1).broadcast_to([P, T, H]),
                                    ALU.subtract).then_inc(diff_ready, 1)
            dve.wait_ge(exp_ready, 2)
            with dve.Fori(0, T) as t:
                v = tile(V, t).rearrange("p (h e) -> p h e", h=H)
                nc.vector.tensor_tensor(v, v, FF[:, bass.ds(t, 1), :].rearrange("p a h -> p (a h)").unsqueeze(2)
                                        .broadcast_to([P, H, DH]), ALU.mult)

        @block.gpsimd
        def _(pool):
            pool.wait_ge(m.adj_loaded, 16 * T * m.adj_loads)
            pool.wait_ge(colmax_ready, 1)
            nc.gpsimd.partition_all_reduce(top[:, :], colmax[:, :], P, RMAX).then_inc(top_ready, 1)

        @block.scalar
        def _(act):
            act.wait_ge(row_ready, 1)
            nc.scalar.activation(c_rows[0:H, :], c_rows[0:H, :], ACT.Exp).then_inc(c_ready, 1)
            act.wait_ge(diff_ready, 1)
            nc.scalar.activation(G[:, :, :], S[:, :, 0:H], ACT.Exp, scale=1.0 - SLOPE).then_inc(exp_ready, 1)
            act.wait_ge(exp_ready, 1)
            nc.scalar.activation(FF[:, :, :], S[:, :, 0:H], ACT.Exp, scale=SLOPE).then_inc(exp_ready, 1)

        @block.sync
        def _(sp):
            sp.wait_ge(c_ready, 1)
            sp.dma_start(c_dram[:, :], c_rows[0:H, :]).then_inc(c_stored, 16)
            sp.wait_ge(c_stored, 16)

    Q = 32
    IB = N // BANK
    nc_ = DH // Q
    nb = nc_ + 1
    cb = core.take(2 * N, m.ring).rearrange("p (u n) -> p u n", u=2)
    Wt = core.take(2 * N).rearrange("p (u n) -> p u n", u=2)
    Pt = core.take(2 * N).rearrange("p (u n) -> p u n", u=2)
    Vs = core.take(2 * (DH + Q), m.w).rearrange("p (u e) -> p u e", u=2)
    ns = core.take(nb * BANK).rearrange("p (b n) -> p b n", b=nb)
    sums = lambda par, b: core.bank(nb * par + b)
    c_in = [sem(f"c_loaded{u}") for u in range(2)]
    relu_done, prob_done, mm_done, fin_done = sem("relu_done"), sem("prob_done"), sem("head_products"), sem("head_done")
    v_ready, ns_ready, turned = sem("values_ready"), sem("sums_moved"), sem("sums_turned")
    fin_s, deg_done = sem("fin_chain"), sem("degree_done")

    def heads_in_pairs(eng, head):
        head(0, 0, False)
        with eng.Fori(0, H // 2 - 1) as p:
            head(p * 2 + 1, 1, True)
            head(p * 2 + 2, 0, True)
        head(H - 1, 1, True)

    with nc.Block() as block:
        @block.sync
        def _(sp):
            with sp.Fori(0, H // 2) as p:
                for u in range(2):
                    sp.wait_ge(relu_done, p * (2 * T) + (u * T + T))
                    sp.dma_start(cb[:, u, :], c_dram[bass.ds(p * 2 + u, 1), :].rearrange("a n -> (a n)")
                                 .partition_broadcast(P)).then_inc(c_in[u], 16)
            sp.wait_ge(c_in[0], 16 * (H // 2))
            sp.wait_ge(c_in[1], 16 * (H // 2))

        @block.gpsimd
        def _(pool):
            with pool.Fori(0, H) as h:
                with pool.Fori(0, T // 2) as q:
                    for v in range(2):
                        n = h * T + q * 2 + v
                        pool.wait_ge(mm_done, n + 1)
                        nc.gpsimd.tensor_copy(Vs[:, v, 0:DH], V[:, bass.ds(q * 2 + v, 1), bass.ds(h * DH, DH)]
                                              .rearrange("p a d -> p (a d)"))
                        nc.gpsimd.tensor_copy(Vs[:, v, DH:DH + Q], FF[:, bass.ds(q * 2 + v, 1), bass.ds(h, 1)]
                                              .rearrange("p a b -> p (a b)").broadcast_to([P, Q])).then_inc(v_ready, 1)

        @block.scalar
        def _(act):
            act.sem_inc(relu_done, 2 * T)

            def head(h, par, before):
                act.wait_ge(c_in[par], (h - par) * 8 + 16)

                def relu(jt, v):
                    act.wait_ge(prob_done, h * T + (jt + 1))
                    g = G[:, bass.ds(jt, 1), bass.ds(h, 1)].rearrange("p a b -> p (a b)")
                    nc.scalar.activation(Wt[:, v], cb[:, par], ACT.Relu, bias=-1.0, scale=g).then_inc(relu_done, 1)

                for jt in range(4):
                    relu(jt, jt % 2)
                if before:
                    move_sums(h - 1, 1 - par)
                with act.Fori(2, T // 2) as q:
                    for v in range(2):
                        relu(q * 2 + v, v)

            def move_sums(h, par):
                act.wait_ge(mm_done, h * T + (T + 2))
                act.wait_ge(turned, h + 1)
                for b in range(nb):
                    last = nc.scalar.activation(ns[:, b], sums(par, b), ACT.Copy)
                last.then_inc(ns_ready, 1)

            heads_in_pairs(act, head)
            move_sums(H - 1, 1)

        @block.vector
        def _(dve):
            dve.sem_inc(prob_done, 2)
            dve.sem_inc(fin_done, 2)

            def finish(h, par):
                dve.wait_ge(turned, h + 2)
                turned_den = sums(par, nc_).rearrange("p (n d) -> p n d", d=Q)
                nc.vector.reciprocal(recip[:, :], turned_den[:, :, 0]).then_inc(fin_s, 1)
                dve.wait_ge(fin_s, h + 1)
                for b in range(nc_):
                    out = hid[:, :, bass.ds(h * DH + b * Q, Q)].rearrange("p (i c) d -> p c i d", i=IB)
                    last = nc.vector.tensor_tensor(
                        out, sums(par, b).rearrange("p (c i d) -> p c i d", i=IB, d=Q),
                        recip.rearrange("p (c i) -> p c i", i=IB).unsqueeze(3).broadcast_to([P, IB, IB, Q]), ALU.mult)
                last.then_inc(fin_done, 1)

            def head(h, par, before):
                def prob(jt, v):
                    dve.wait_ge(relu_done, h * T + (jt + 1 + 2 * T))
                    dve.wait_ge(mm_done, h * T + (jt + 1))
                    nc.vector.scalar_tensor_tensor(Pt[:, v], Wt[:, v], 1.0, tile(m.adj, jt), ALU.add, ALU.mult) \
                        .then_inc(prob_done, 1)

                for jt in range(6):
                    prob(jt, jt % 2)
                if before:
                    finish(h - 1, 1 - par)
                with dve.Fori(3, T // 2) as q:
                    for v in range(2):
                        prob(q * 2 + v, v)

            heads_in_pairs(dve, head)
            finish(H - 1, 1)
            if degree:
                dve.wait_ge(deg_done, 1)
                link = Chain(dve, fin_s, H)
                link(nc.vector.tensor_scalar(m.rdeg[:, :], core.bank(7)[:, 0:T], 1.0, 1e-12, ALU.add, ALU.max))
                link(nc.vector.reciprocal(m.rdeg[:, :], m.rdeg[:, :]))

        @block.tensor
        def _(pe):
            pe.sem_inc(mm_done, 2)
            pe.sem_inc(turned, 1)

            def turn(h, par):
                pe.wait_ge(ns_ready, h + 1)
                for b in range(nb):
                    for c in range(IB):
                        last = nc.tensor.transpose(sums(par, b)[:, c * P:(c + 1) * P], ns[:, b, c * P:(c + 1) * P],
                                                   m.ident[:, :])
                last.then_inc(turned, 1)

            def head(h, par, before):
                def products(jt, v):
                    pe.wait_ge(prob_done, h * T + (jt + 3))
                    pe.wait_ge(v_ready, h * T + (jt + 1))
                    for b in range(nb):
                        for i in range(IB):
                            last = nc.tensor.matmul(sums(par, b)[i * Q:(i + 1) * Q, :], Vs[:, v, b * Q:(b + 1) * Q],
                                                    Pt[:, v, i * BANK:(i + 1) * BANK], start=False, stop=False,
                                                    skip_group_check=True)
                    last.then_inc(mm_done, 1)

                pe.wait_ge(fin_done, h + 1)
                for b in range(nb):
                    nc.tensor.matmul(sums(par, b), m.zeros[:, 0:P], m.zeros[:, :], start=True, stop=False,
                                     skip_group_check=True)
                for jt in range(4):
                    products(jt, jt % 2)
                if before:
                    turn(h - 1, 1 - par)
                with pe.Fori(2, T // 2) as q:
                    for v in range(2):
                        products(q * 2 + v, v)

            heads_in_pairs(pe, head)
            turn(H - 1, 1)
            if degree:
                for it in range(T):
                    last = accumulate(nc, core.bank(7)[:, it:it + 1],
                                      [(m.adj[:, jt, it * P:(it + 1) * P], m.ones[:, 0:1]) for jt in range(T)])
                last.then_inc(deg_done, 1)
    return hid


def mix_out(core, m, tag, hid, x_dram, w_dram, b_dram, y_dram):
    nc = core.nc
    sem = lambda n: core.sem(f"{tag}_{n}")
    X = core.take(T * D, m.ring).rearrange("p (t d) -> p t d", t=T)
    hs = core.take(2 * D).rearrange("p (u d) -> p u d", u=2)
    hT = core.take(2 * D).rearrange("p (u k n) -> p u k n", u=2, k=KD)
    W = core.take(KD * D, m.w).rearrange("p (k d) -> p k d", k=KD)
    b = core.take(D)
    yb, lo, ex, o = (core.take(2 * D, m.big_c + 2 * D * n).rearrange("p (u d) -> p u d", u=2) for n in range(4))
    loaded = sem("loaded")
    h_ready, t_done, ht_ready, mm_done = sem("h_ready"), sem("transposed"), sem("hT_ready"), sem("projected")
    vec, lo_ready, ex_ready, o_ready, stored = sem("v_chain"), sem("lo_ready"), sem("exp_ready"), sem("o_ready"), sem("stored")
    biased = sem("biased")
    with nc.Block() as block:
        @block.sync
        def _(sp):
            sp.dma_start(X[:, :, :], x_dram.rearrange("t p d -> p t d")).then_inc(loaded, 16)
            sp.dma_start(W[:, :, :], w_dram).then_inc(loaded, 16)
            sp.dma_start(b[:, :], b_dram).then_inc(loaded, 16)
            sp.sem_inc(stored, 32)
            with sp.Fori(0, T) as t:
                sp.wait_ge(o_ready, t + 1)
                sp.dma_start(rows(y_dram, t), tile(X, t)).then_inc(stored, 16)
            sp.wait_ge(stored, 16 * T + 32)

        @block.scalar
        def _(act):
            with act.Fori(0, T // 2) as p:
                for u in range(2):
                    act.wait_ge(t_done, p * 2 + (u + 1))
                    nc.scalar.activation(hs[:, u], tile(hid, p * 2 + u), ACT.Copy).then_inc(h_ready, 1)
                for u in range(2):
                    act.wait_ge(lo_ready, p * 2 + (u + 1))
                    nc.scalar.activation(ex[:, u], lo[:, u], ACT.Exp).then_inc(ex_ready, 1)

        @block.tensor
        def _(pe):
            pe.wait_ge(loaded, 48)
            pe.sem_inc(t_done, 2)
            pe.sem_inc(mm_done, 2)
            with pe.Fori(0, T // 2) as p:
                for u in range(2):
                    pe.wait_ge(h_ready, p * 2 + (u + 1))
                    pe.wait_ge(ht_ready, p * 2 + (u + 1))
                    for k in range(KD):
                        last = nc.tensor.transpose(core.bank(u)[:, k * P:(k + 1) * P],
                                                   hs[:, u, k * P:(k + 1) * P], m.ident[:, :])
                    last.then_inc(t_done, 1)
                for u in range(2):
                    pe.wait_ge(ht_ready, p * 2 + (u + 3))
                    pe.wait_ge(biased, p * 2 + (u + 1))
                    accumulate(nc, core.bank(2 + u), [(hT[:, u, k], W[:, k]) for k in range(KD)]).then_inc(mm_done, 1)

        @block.vector
        def _(dve):
            dve.sem_inc(ht_ready, 2)
            dve.sem_inc(biased, 2)
            dve.wait_ge(loaded, 48)
            with dve.Fori(0, T // 2) as p:
                for u in range(2):
                    dve.wait_ge(t_done, p * 2 + (u + 3))
                    dve.wait_ge(mm_done, p * 2 + (u + 1))
                    nc.vector.tensor_copy(hT[:, u], core.bank(u).rearrange("p (k n) -> p k n", k=KD)) \
                        .then_inc(ht_ready, 1)
                for u in range(2):
                    dve.wait_ge(mm_done, p * 2 + (u + 3))
                    nc.vector.tensor_tensor(yb[:, u], core.bank(2 + u), b[:, :], ALU.add).then_inc(biased, 1)
                    dve.wait_ge(biased, p * 2 + (u + 3))
                    nc.vector.tensor_scalar_min(lo[:, u], yb[:, u], 0.0).then_inc(lo_ready, 1)
                for u in range(2):
                    link = Chain(dve, vec, p * 2 + u)
                    dve.wait_ge(ex_ready, p * 2 + (u + 1))
                    link(nc.vector.scalar_tensor_tensor(o[:, u], yb[:, u], 0.0, ex[:, u], ALU.max, ALU.add))
                    nc.vector.scalar_tensor_tensor(tile(X, p * 2 + u), o[:, u], -1.0, tile(X, p * 2 + u),
                                                   ALU.add, ALU.add).then_inc(o_ready, 1)


def nucleus_front(core, m, x_dram, w1t_dram, w2_dram, w3_dram, h_dram):
    nc = core.nc
    A = W2N
    W3 = core.take(KD * A, m.w).rearrange("p (k a) -> p k a", k=KD)
    W12 = core.take(KD * A).rearrange("p (k a) -> p k a", k=KD)
    W1T, W2 = core.take(D), core.take(A)
    XA = core.take(T * D, m.big_b).rearrange("p (t d) -> p t d", t=T)
    KQ = core.take(2 * N, T * D).rearrange("p (s n) -> p s n", s=2)
    folded, stored = core.sem("nf_folded"), core.sem("nf_stored")

    def project(nc, hT, u):
        accumulate(nc, core.bank(2 + u)[0:A, 0:P], [(W3[:, k], hT[:, k]) for k in range(KD)])
        return accumulate(nc, core.bank(2 + u)[0:A, P:2 * P], [(W12[:, k], hT[:, k]) for k in range(KD)])

    def evac_dve(nc, t, u):
        return nc.vector.tensor_copy(KQ[0:A, :, bass.ds(t * P, P)],
                                     core.bank(2 + u)[0:A, 0:2 * P].rearrange("p (s n) -> p s n", s=2))

    fold_in = core.sem("nf_fold_loaded")
    with nc.Block() as block:
        @block.sync
        def _(sp):
            sp.dma_start(W1T[0:A, :], w1t_dram).then_inc(fold_in, 16)
            sp.dma_start(W2[0:A, :], w2_dram).then_inc(fold_in, 16)

        @block.tensor
        def _(pe):
            pe.wait_ge(fold_in, 32)
            for k in range(KD):
                last = nc.tensor.matmul(core.bank(6)[:, k * A:(k + 1) * A], W1T[0:A, k * P:(k + 1) * P], W2[0:A, :],
                                        start=True, stop=True)
            last.then_inc(folded, 1)

        @block.vector
        def _(dve):
            dve.wait_ge(folded, 1)
            nc.vector.tensor_copy(W12[:, :, :], core.bank(6)[:, 0:KD * A].rearrange("p (k a) -> p k a", k=KD))

    front(core, m, "nf", x_dram, [(W3[:, :, :], w3_dram)], project=project, evac_dve=evac_dve, natural=XA)
    with nc.Block() as block:
        @block.sync
        def _(sp):
            sp.dma_start(h_dram.rearrange("t p d -> p t d"), XA[:, :, :]).then_inc(stored, 16)
            sp.wait_ge(stored, 16)
    return XA, KQ, W3, W12


def tiles_ahead(eng, before, at):
    before(0, 0)
    with eng.Fori(0, T // 2 - 1) as p:
        before(p * 2 + 1, 1)
        at(p * 2, 0)
        before(p * 2 + 2, 0)
        at(p * 2 + 1, 1)
    before(T - 1, 1)
    at(T - 2, 0)
    at(T - 1, 1)


def nucleus_step(core, m, tag, XA, XF, KQ, adjT, xa_out, xf_out):
    nc = core.nc
    sem = lambda n: core.sem(f"{tag}_{n}")
    E = core.take(2 * N, m.ring).rearrange("p (u n) -> p u n", u=2)
    b = core.take(2 * N).rearrange("p (u n) -> p u n", u=2)
    A = core.take(N)
    AT = core.take(N).rearrange("p (t n) -> p t n", t=T)
    C = core.take(N + 4, m.big_c)
    adj = core.take(N).rearrange("p (t n) -> p t n", t=T)
    xas, xfs = core.take(D), core.take(D)
    ramp = core.take(S_COLS).bitcast(BF16).rearrange("p (u n) -> p u n", u=2)
    sign = core.take(S_COLS).bitcast(BF16).rearrange("p (u n) -> p u n", u=2)
    qs = core.take(P, m.free)
    small = core.take(32)
    mx, nmax, Z1, Z2, rest, goal, mid, got, r, s, q = (small[:, 2 * n:2 * n + 2] for n in range(11))
    aim, low, high, all_, left, cut, S, rS, s_cols = (small[:, n:n + 1] for n in range(22, 31))
    q_ready, l_done, max_done, nmax_ready, e_ready = (sem(n) for n in ("q", "logits", "max", "minus_max", "exp"))
    adj_in, r_done, a_ready, t_done, t_moved = (sem(n) for n in ("adj", "r_product", "nucleus", "turned", "turned_moved"))
    m_done, s_done, xa_ready, xa_stored, rs_ready = (sem(n) for n in ("a_product", "searched", "xa", "xa_stored", "a_sum"))
    xf_moved, xf_chain, xf_ready, xf_stored, vec = (sem(n) for n in ("xf_moved", "xf_sum", "xf", "xf_stored", "v_chain"))
    mid_ready, got_ready, acc_ready, ends_ready, cut_ready, gp = (sem(n) for n in (
        "mid", "v_sum", "s_sums", "interval", "cut", "g_chain"))
    G = 4
    NG = T // G
    lbank, rbank, mbank = core.bank(0, 4), core.bank(7), core.bank(6)
    HALF = HALVINGS // 2
    ratio = lambda h: math.exp(DEPTH / 2 ** (h + 2))
    SLACK = 4e-6
    first_mid = lambda i: i * (2 * HALF + 1) + HALF + 2
    first_sum = lambda i: i * (2 * HALF) + HALF

    def rounds(eng, body):
        body(0, 0)
        with eng.Fori(0, (T - 4) // 2) as p:
            body(p * 2 + 1, 1)
            body(p * 2 + 2, 0)
        for i in range(T - 3, T):
            body(i, i % 2)

    fixed = lambda i, n: type(i) is int and i == n
    beyond = lambda i, n: type(i) is int and i >= n

    def halvings(i, u, step):
        for h in range(HALF):
            if fixed(i, T - 1):
                yield step(u, HALF + h, h)
            else:
                yield step(u, HALF + h, 2 * h)
                yield step(1 - u, h, 2 * h + 1)

    def halving_mid(i, n):
        return first_mid(i) + (n if fixed(i, T - 1) else n - 1)

    with nc.Block() as block:
        @block.sync
        def _(sp):
            def load(i, u):
                sp.wait_ge(r_done, i + 1)
                sp.dma_start(adj[:, :, :], adjT[:, :, bass.ds(i * P, P)].rearrange("t p n -> p t n")) \
                    .then_inc(adj_in, 16)

            def store(i, u):
                sp.wait_ge(xf_ready, i + 1)
                sp.dma_start(rows(xf_out, i), xfs[:, :]).then_inc(xf_stored, 16)
                sp.wait_ge(xa_ready, i + 2)
                sp.dma_start(rows(xa_out, i), xas[:, :]).then_inc(xa_stored, 16)

            sp.sem_inc(xf_stored, 16)
            sp.sem_inc(xa_stored, 16)
            tiles_ahead(sp, load, store)
            sp.wait_ge(xf_stored, 16 * (T + 1))
            sp.wait_ge(xa_stored, 16 * (T + 1))

        @block.tensor
        def _(pe):
            def logits(i):
                pe.wait_ge(q_ready, i + 1)
                if not fixed(i, 0):
                    pe.wait_ge(e_ready, i * 2)
                for c in range(N // BANK):
                    last = nc.tensor.matmul(core.bank(c), qs[0:W2N, :], KQ[0:W2N, 0, c * BANK:(c + 1) * BANK],
                                            start=True, stop=True)
                last.then_inc(l_done, 1)

            def r_product(i):
                pe.wait_ge(adj_in, i * 16 + 16)
                pe.wait_ge(xf_moved, i + 1)
                accumulate(nc, rbank, [(adj[:, jt], XF[:, jt]) for jt in range(T)]).then_inc(r_done, 1)

            def a_product(i):
                pe.wait_ge(a_ready, i + 1)
                for g in range(NG):
                    pe.wait_ge(t_moved, i * NG + (g + 1))
                    for c in range(G):
                        last = nc.tensor.transpose(core.bank(4 + g % 2)[:, c * P:(c + 1) * P],
                                                   A[:, (g * G + c) * P:(g * G + c + 1) * P], m.ident[:, :])
                    last.then_inc(t_done, 1)
                pe.wait_ge(t_moved, i * NG + (NG + 2))
                pe.wait_ge(xa_ready, i + 1)
                accumulate(nc, mbank, [(AT[:, jt], XA[:, jt]) for jt in range(T)]).then_inc(m_done, 1)

            def body(i, u):
                if not beyond(i, T - 2):
                    logits(i + 2)
                if not fixed(i, 0):
                    a_product(i - 1)
                r_product(i)

            pe.sem_inc(l_done, 1)
            pe.sem_inc(r_done, 1)
            pe.sem_inc(m_done, 1)
            pe.sem_inc(t_done, 1)
            logits(0)
            logits(1)
            rounds(pe, body)
            a_product(T - 1)

        @block.scalar
        def _(act):
            def query(i):
                act.wait_ge(l_done, i + 1)
                nc.scalar.activation(qs[0:W2N, :], KQ[0:W2N, 1, bass.ds(i * P, P)], ACT.Copy).then_inc(q_ready, 1)

            def exps(i, u):
                act.wait_ge(s_done, i + 1)
                act.wait_ge(nmax_ready, i + 1)
                for part, Z in ((slice(0, V_COLS), Z1), (slice(V_COLS, N), Z2)):
                    nc.scalar.activation(E[:, u, part], lbank[:, part], ACT.Exp, bias=nmax[:, u:u + 1],
                                         accum_out=Z[:, u:u + 1]).then_inc(e_ready, 1)

            def sums(u, mids):
                act.wait_ge(mid_ready, mids)
                for func, out, total in ((ACT.Relu, ramp, r), (ACT.Sign, sign, s)):
                    nc.scalar.activation(out[:, u, :], E[:, u, V_COLS:N], func, bias=mid[:, u:u + 1], scale=-1.0,
                                         accum_out=total[:, u:u + 1]).then_inc(acc_ready, 1)

            def move_xf(i):
                act.wait_ge(r_done, i + 2)
                act.wait_ge(xf_stored, i * 16 + 16)
                nc.scalar.activation(xfs[:, :], rbank, ACT.Copy).then_inc(xf_moved, 1)

            def move_turned(i):
                act.wait_ge(m_done, i + 1)
                for g in range(NG):
                    act.wait_ge(t_done, i * NG + (g + 2))
                    nc.scalar.activation(AT[:, g * G:(g + 1) * G, :],
                                         core.bank(4 + g % 2).rearrange("p (c n) -> p c n", c=G), ACT.Copy) \
                        .then_inc(t_moved, 1)

            def move_xa(i):
                act.wait_ge(m_done, i + 2)
                act.wait_ge(rs_ready, i + 1)
                act.wait_ge(xa_stored, i * 16 + 16)
                nc.scalar.activation(xas[:, :], mbank, ACT.Copy, scale=rS).then_inc(xa_ready, 1)

            def body(i, u):
                if not beyond(i, T - 2):
                    query(i + 2)
                for n, _ in enumerate(halvings(i, u, lambda slot, h, n: sums(slot, halving_mid(i, n)))):
                    if n == 1 and not fixed(i, 0):
                        move_xf(i - 1)
                    if n == 3 and not fixed(i, 0):
                        move_turned(i - 1)
                if not beyond(i, T - 2):
                    exps(i + 2, u)
                if not fixed(i, 0):
                    move_xa(i - 1)

            act.sem_inc(t_moved, 2)
            act.sem_inc(xf_moved, 1)
            act.sem_inc(xa_ready, 1)
            query(0)
            query(1)
            exps(0, 0)
            for h in range(HALF):
                sums(0, h + 1)
            exps(1, 1)
            rounds(act, body)
            move_xf(T - 1)
            move_turned(T - 1)
            move_xa(T - 1)

        @block.gpsimd
        def _(pool):
            def start(i, u):
                c = slice(u, u + 1)
                pool.wait_ge(e_ready, i * 2 + 2)
                nc.gpsimd.tensor_tensor(goal[:, c], Z1[:, c], Z2[:, c], ALU.add).then_inc(gp, 1)
                pool.wait_ge(gp, 1)
                nc.gpsimd.tensor_scalar(mid[:, c], goal[:, c], 0.0, math.exp(-DEPTH / 2), ALU.mult, ALU.add) \
                    .then_inc(gp, 1)
                pool.wait_ge(gp, 2)
                nc.gpsimd.tensor_scalar(goal[:, c], goal[:, c], TOP_P, None, ALU.mult).then_inc(gp, 1)
                pool.wait_ge(gp, 3)
                nc.gpsimd.tensor_tensor(rest[:, c], goal[:, c], Z2[:, c], ALU.subtract).then_inc(mid_ready, 1)
                pool.sem_clear(gp)

            def move_mid(u, h, sums):
                c = slice(u, u + 1)
                up, down = ratio(h), 1 / ratio(h)
                pool.wait_ge(acc_ready, sums * 2)
                pool.wait_ge(got_ready, sums)
                nc.gpsimd.tensor_tensor(q[:, c], s[:, c], s_cols, ALU.add).then_inc(gp, 1)
                pool.wait_ge(gp, 1)
                nc.gpsimd.tensor_scalar(q[:, c], q[:, c], mid[:, c], -0.5, ALU.mult, ALU.mult).then_inc(gp, 1)
                pool.wait_ge(gp, 2)
                nc.gpsimd.tensor_scalar(q[:, c], q[:, c], r[:, c], got[:, c], ALU.add, ALU.add).then_inc(gp, 1)
                pool.wait_ge(gp, 3)
                nc.gpsimd.tensor_scalar(q[:, c], q[:, c], rest[:, c], up - down, ALU.is_ge, ALU.mult).then_inc(gp, 1)
                pool.wait_ge(gp, 4)
                nc.gpsimd.tensor_scalar(mid[:, c], q[:, c], down, mid[:, c], ALU.add, ALU.mult).then_inc(mid_ready, 1)
                pool.sem_clear(gp)

            def body(i, u):
                for n, _ in enumerate(halvings(i, u, lambda slot, h, n: move_mid(slot, h, first_sum(i) + (n + 1)))):
                    if n == 3 and not fixed(i, 0):
                        xf_sum(i - 1)
                if not beyond(i, T - 2):
                    pool.wait_ge(ends_ready, i * 2 + 3)
                    start(i + 2, u)
                elif fixed(i, T - 2):
                    pool.sem_inc(mid_ready, 1)
                pool.wait_ge(cut_ready, i + 1)
                nc.gpsimd.tensor_tensor(A[:, :], A[:, :], b[:, u, :], ALU.subtract).then_inc(a_ready, 1)

            def xf_sum(i):
                pool.wait_ge(xf_moved, i + 2)
                nc.gpsimd.tensor_tensor(xfs[:, :], xfs[:, :], tile(XF, i), ALU.add).then_inc(xf_chain, 1)
                pool.wait_ge(xf_chain, i + 1)
                nc.gpsimd.tensor_tensor(xfs[:, :], xfs[:, :], cols(m.rdeg, i, 1).broadcast_to([P, D]), ALU.mult) \
                    .then_inc(xf_ready, 1)

            nc.gpsimd.memset(s_cols, float(S_COLS)).then_inc(ends_ready, 1)
            pool.wait_ge(ends_ready, 1)
            start(0, 0)
            for h in range(HALF):
                move_mid(0, h, h + 1)
            start(1, 1)
            rounds(pool, body)
            xf_sum(T - 1)

        @block.vector
        def _(dve):
            PER = 8

            def rowmax(i, u):
                dve.wait_ge(l_done, i + 2)
                nc.vector.tensor_reduce(mx[:, u:u + 1], lbank, AX.X, ALU.max).then_inc(max_done, 1)
                dve.wait_ge(max_done, i + 1)
                nc.vector.tensor_scalar(nmax[:, u:u + 1], mx[:, u:u + 1], -1.0, None, ALU.mult).then_inc(nmax_ready, 1)

            def summed(u, mids):
                dve.wait_ge(mid_ready, mids)
                nc.vector.scalar_tensor_tensor(b[:, u, 0:V_COLS], E[:, u, 0:V_COLS], mid[:, u:u + 1],
                                               E[:, u, 0:V_COLS], ALU.is_gt, ALU.mult, accum_out=got[:, u:u + 1]) \
                    .then_inc(got_ready, 1)

            def nucleus(i, u, mids):
                link = Chain(dve, vec, i * PER)
                end, c = ratio(HALVINGS - 1), slice(u, u + 1)
                dve.wait_ge(mid_ready, mids)
                nc.vector.tensor_scalar(high, mid[:, c], end * (1 + SLACK), None, ALU.mult).then_inc(ends_ready, 1)
                nc.vector.tensor_copy(aim, goal[:, c]).then_inc(ends_ready, 1)
                link(nc.vector.tensor_scalar(low, mid[:, c], (1 - SLACK) / end, None, ALU.mult))
                dve.wait_ge(t_done, i * NG + 1)
                link(nc.vector.scalar_tensor_tensor(A[:, :], E[:, u, :], low, E[:, u, :], ALU.is_gt, ALU.mult,
                                                    accum_out=all_))
                dve.sem_inc(s_done, 1)
                dve.wait_ge(ends_ready, i * 2 + 3)
                link(nc.vector.scalar_tensor_tensor(b[:, u, :], A[:, :], high, A[:, :], ALU.is_le, ALU.mult,
                                                    accum_out=left))
                link(nc.vector.tensor_tensor(C[:, 0:1], all_, left, ALU.subtract))
                link(nc.vector.tensor_tensor_scan(C[:, 1:N + 1], b[:, u, :], b[:, u, :], C[:, 0:1], ALU.add, ALU.max))
                link(nc.vector.scalar_tensor_tensor(b[:, u, :], C[:, 0:N], aim, b[:, u, :], ALU.is_ge, ALU.mult,
                                                    accum_out=cut))
                dve.sem_inc(cut_ready, 1)
                link(nc.vector.tensor_tensor(S, all_, cut, ALU.subtract))
                dve.wait_ge(xa_ready, i + 1)
                link(nc.vector.reciprocal(rS, S))
                dve.sem_inc(rs_ready, 1)
                assert link.k == PER, link.k

            def body(i, u):
                for n, _ in enumerate(halvings(i, u, lambda slot, h, n: summed(slot, halving_mid(i, n)))):
                    if n == 0 and not fixed(i, 0):
                        dve.wait_ge(a_ready, i)
                    if n == 7 and not beyond(i, T - 2):
                        rowmax(i + 2, u)
                nucleus(i, u, first_mid(i) + (HALF if fixed(i, T - 1) else 2 * HALF - 1))

            dve.sem_inc(s_done, 2)
            rowmax(0, 0)
            rowmax(1, 1)
            for h in range(HALF):
                summed(0, h + 1)
            rounds(dve, body)


def nucleus_sum(core, m, tag, xa_dram, xf_dram, y_dram, u1_dram, u2_dram, W3, W12, y_out):
    nc = core.nc
    sem = lambda n: core.sem(f"{tag}_{n}")
    again = y_out is not None
    XA = core.take(T * D, m.big_b).rearrange("p (t d) -> p t d", t=T)
    XF = core.take(T * D, 0).rearrange("p (t d) -> p t d", t=T)
    KQ = core.take(2 * N).rearrange("p (s n) -> p s n", s=2)
    Y = core.take(T * D, m.ring).rearrange("p (t d) -> p t d", t=T)
    hs = core.take(4 * D).rearrange("p (u d) -> p u d", u=4)
    U = core.take(2 * KD * D, m.big_c).rearrange("p (s k d) -> p s k d", s=2, k=KD)
    hT = core.take(4 * D).rearrange("p (u k n) -> p u k n", u=4, k=KD)
    loaded, y_in = sem("loaded"), sem("y_loaded")
    h_ready, t_done, ht_ready, mm_done, y_ready, stored = (sem(n) for n in ("h", "turned", "hT", "products", "y", "stored"))
    with nc.Block() as block:
        @block.sync
        def _(sp):
            for dst, src in ((U[:, 0], u1_dram), (U[:, 1], u2_dram), (XF[:, :, :], xf_dram.rearrange("t p d -> p t d")),
                             (XA[:, :, :], xa_dram.rearrange("t p d -> p t d"))):
                sp.dma_start(dst, src).then_inc(loaded, 16)
            sp.dma_start(Y[:, :, :], y_dram.rearrange("t p d -> p t d")).then_inc(y_in, 16)
            if again:
                with sp.Fori(0, T) as t:
                    sp.wait_ge(y_ready, t + 3)
                    sp.dma_start(rows(y_out, t), tile(Y, t)).then_inc(stored, 16)
                sp.wait_ge(stored, 16 * T)

        @block.scalar
        def _(act):
            act.wait_ge(loaded, 64)
            with act.Fori(0, T // 2) as p:
                for u in range(2):
                    act.wait_ge(t_done, p * 2 + (u + 1))
                    nc.scalar.activation(hs[:, 2 * u], tile(XF, p * 2 + u), ACT.Copy)
                    nc.scalar.activation(hs[:, 2 * u + 1], tile(XA, p * 2 + u), ACT.Copy).then_inc(h_ready, 1)

        @block.tensor
        def _(pe):
            pe.wait_ge(loaded, 64)
            pe.sem_inc(t_done, 2)
            pe.sem_inc(mm_done, 2)
            with pe.Fori(0, T // 2) as p:
                for u in range(2):
                    pe.wait_ge(h_ready, p * 2 + (u + 1))
                    pe.wait_ge(ht_ready, p * 2 + (u + 1))
                    for s in range(2):
                        for k in range(KD):
                            last = nc.tensor.transpose(core.bank(2 * u + s)[:, k * P:(k + 1) * P],
                                                       hs[:, 2 * u + s, k * P:(k + 1) * P], m.ident[:, :])
                    last.then_inc(t_done, 1)
                for u in range(2):
                    pe.wait_ge(ht_ready, p * 2 + (u + 3))
                    pe.wait_ge(y_ready, p * 2 + (u + 1))
                    last = accumulate(nc, core.bank(4 + u), [(hT[:, 2 * u + s, k], U[:, s, k])
                                                             for s in range(2) for k in range(KD)])
                    if again:
                        for s, w in enumerate((W3, W12)):
                            last = accumulate(nc, core.bank(6 + u)[0:W2N, s * P:(s + 1) * P],
                                              [(w[:, k], hT[:, 2 * u + 1, k]) for k in range(KD)])
                    last.then_inc(mm_done, 1)

        @block.vector
        def _(dve):
            dve.sem_inc(ht_ready, 2)
            dve.sem_inc(y_ready, 2)
            dve.wait_ge(y_in, 16)
            with dve.Fori(0, T // 2) as p:
                for u in range(2):
                    dve.wait_ge(t_done, p * 2 + (u + 3))
                    dve.wait_ge(mm_done, p * 2 + (u + 1))
                    nc.vector.tensor_copy(hT[:, 2 * u:2 * u + 2].rearrange("p u k n -> p (u k n)"),
                                          core.bank(2 * u, 2)).then_inc(ht_ready, 1)
                for u in range(2):
                    dve.wait_ge(mm_done, p * 2 + (u + 3))
                    if again:
                        nc.vector.tensor_copy(KQ[0:W2N, :, bass.ds((p * 2 + u) * P, P)],
                                              core.bank(6 + u)[0:W2N, 0:2 * P].rearrange("p (s n) -> p s n", s=2))
                    y = tile(Y, p * 2 + u)
                    nc.vector.tensor_tensor(y, core.bank(4 + u), y, ALU.add).then_inc(y_ready, 1)
    return XA, XF, KQ, Y


def nucleus_out(core, m, Y, x_dram, gamma_dram, beta_dram, out_dram):
    nc = core.nc
    sem = lambda n: core.sem(f"no_{n}")
    X = core.take(T * D, m.big_b).rearrange("p (t d) -> p t d", t=T)
    gamma, beta = core.take(D, m.big_c), core.take(D)
    n1 = core.take(2 * D).rearrange("p (u d) -> p u d", u=2)
    loaded, vec, stats, root, ready, stored, scaled, used = (sem(n) for n in (
        "loaded", "v_chain", "variance", "root", "out_ready", "stored", "scaled", "used"))
    pool_chain = sem("pool_chain")
    with nc.Block() as block:
        @block.sync
        def _(sp):
            for dst, src in ((gamma[:, :], gamma_dram), (beta[:, :], beta_dram),
                             (X[:, :, :], x_dram.rearrange("t p d -> p t d"))):
                sp.dma_start(dst, src).then_inc(loaded, 16)
            with sp.Fori(0, T) as t:
                sp.wait_ge(ready, t + 1)
                sp.dma_start(rows(out_dram, t), tile(X, t)).then_inc(stored, 16)
            sp.wait_ge(stored, 16 * T)

        @block.scalar
        def _(act):
            act.wait_ge(stats, 1)
            nc.scalar.activation(m.std[:, :], m.var[:, :], ACT.Sqrt).then_inc(root, 1)

        @block.gpsimd
        def _(pool):
            pool.wait_ge(loaded, 48)
            with pool.Fori(0, T) as t:
                nc.gpsimd.tensor_tensor(tile(X, t), tile(X, t), beta[:, :], ALU.add).then_inc(used, 1)

        @block.vector
        def _(dve):
            link = Chain(dve, vec)
            for t in range(T):
                link(nc.vector.bn_stats(m.st[:, :], Y[:, t]))
                link(nc.vector.bn_aggr(m.mv[:, t], m.st[:, :]))
            nc.vector.tensor_scalar_add(m.var[:, :], m.mv[:, :, 1], LN_EPS).then_inc(stats, 1)
            dve.wait_ge(root, 1)
            link(nc.vector.reciprocal(m.rstd[:, :], m.std[:, :]))
            dve.wait_ge(loaded, 48)
            with dve.Fori(0, T) as t:
                step = Chain(dve, vec, t * 2 + link.k)
                mean = m.mv[:, bass.ds(t, 1), 0:1].rearrange("p a b -> p (a b)")
                step(nc.vector.tensor_scalar(n1[:, 0], tile(Y, t), mean, cols(m.rstd, t, 1), ALU.subtract, ALU.mult))
                step(nc.vector.tensor_tensor(n1[:, 1], n1[:, 0], gamma[:, :], ALU.mult))
                dve.wait_ge(used, t + 1)
                nc.vector.tensor_tensor(tile(X, t), tile(X, t), n1[:, 1], ALU.add).then_inc(ready, 1)


def dot_attention(core, m, x_dram, adj_dram, weights, biases, x_out):
    nc = core.nc
    sem = lambda n: core.sem(f"dot_{n}")
    W = [core.take(KD * D, n * KD * D).rearrange("p (k d) -> p k d", k=KD) for n in range(3)]
    kT = core.take(T * D, T * D).rearrange("p (k n) -> p k n", k=KD)
    qT = core.take(T * D, m.big_b).rearrange("p (k n) -> p k n", k=KD)
    V = core.take(T * D, m.big_c).rearrange("p (t d) -> p t d", t=T)
    bv, bq, bk = core.take(D, m.w), core.take(KD), core.take(KD)

    def project(nc, hT, u):
        for n in range(2):
            for c in range(KD):
                accumulate(nc, core.bank(2 + u + 2 * n)[:, c * P:(c + 1) * P],
                           [(W[n][:, k, c * P:(c + 1) * P], hT[:, k]) for k in range(KD)])
        return accumulate(nc, core.bank(6 + u), [(hT[:, k], W[2][:, k]) for k in range(KD)])

    def evac_dve(nc, t, u):
        for n, (dst, bias) in enumerate(((qT, bq), (kT, bk))):
            nc.vector.tensor_tensor(dst[:, :, bass.ds(t * P, P)], core.bank(2 + u + 2 * n).rearrange("p (k n) -> p k n", k=KD),
                                    bias.unsqueeze(2).broadcast_to([P, KD, P]), ALU.add)
        return nc.vector.tensor_tensor(tile(V, t), core.bank(6 + u), bv[:, :], ALU.add)

    front(core, m, "dot", x_dram, [(w[:, :, :], d) for w, d in zip(W, weights)]
          + [(bq[:, :], biases[0]), (bk[:, :], biases[1]), (bv[:, :], biases[2])], project=project, evac_dve=evac_dve)

    adj = core.take(2 * N, m.ring).rearrange("p (u n) -> p u n", u=2)
    s, b, A = core.take(N), core.take(N), core.take(N)
    AT = core.take(N).rearrange("p (t n) -> p t n", t=T)
    qs = core.take(D, 0).rearrange("p (k n) -> p k n", k=KD)
    xt = core.take(2 * D).rearrange("p (u d) -> p u d", u=2)
    o = core.take(D)
    small = core.take(8)
    mx, nmax, Z, rZ = (small[:, n:n + 1] for n in range(4))
    G, NG = 4, T // 4
    SCALE = 1.0 / float(D) ** 0.5
    lbank, mbank = core.bank(0, 4), core.bank(6)
    adj_in, x_in = [sem(f"adj{u}") for u in range(2)], [sem(f"x{u}") for u in range(2)]
    q_ready, l_done, l_read, max_ready, e_ready, t_done, t_moved, m_done, o_ready, stored, vec, r_ready = (
        sem(n) for n in ("q", "logits", "logits_read", "max", "exp", "turned", "turned_moved", "product", "out",
                         "stored", "v_chain", "reciprocal"))

    with nc.Block() as block:
        @block.sync
        def _(sp):
            def load(i, u):
                sp.wait_ge(o_ready, i + 1)
                sp.dma_start(adj[:, u], rows(adj_dram, i)).then_inc(adj_in[u], 16)
                sp.dma_start(xt[:, u], rows(x_dram, i)).then_inc(x_in[u], 16)

            def store(i, u):
                sp.wait_ge(o_ready, i + 3)
                sp.dma_start(rows(x_out, i), xt[:, u]).then_inc(stored, 16)
                sp.wait_ge(stored, i * 16 + 16)

            load(0, 0)
            load(1, 1)
            with sp.Fori(0, T // 2 - 1) as p:
                for u in range(2):
                    store(p * 2 + u, u)
                    load(p * 2 + (u + 2), u)
            store(T - 2, 0)
            store(T - 1, 1)

        @block.tensor
        def _(pe):
            def logits(i, u):
                pe.wait_ge(q_ready, i + 1)
                pe.wait_ge(l_read, i + 1)
                for c in range(N // BANK):
                    last = accumulate(nc, core.bank(c), [(qs[:, k], kT[:, k, c * BANK:(c + 1) * BANK]) for k in range(KD)])
                last.then_inc(l_done, 1)

            def product(i, u):
                pe.wait_ge(e_ready, i + 1)
                for g in range(NG):
                    pe.wait_ge(t_moved, i * NG + (g + 1))
                    for c in range(G):
                        last = nc.tensor.transpose(core.bank(4 + g % 2)[:, c * P:(c + 1) * P],
                                                   A[:, (g * G + c) * P:(g * G + c + 1) * P], m.ident[:, :])
                    last.then_inc(t_done, 1)
                pe.wait_ge(t_moved, i * NG + (NG + 2))
                pe.wait_ge(o_ready, i + 2)
                accumulate(nc, mbank, [(AT[:, jt], V[:, jt]) for jt in range(T)]).then_inc(m_done, 1)

            pe.sem_inc(l_done, 1)
            pe.sem_inc(m_done, 1)
            pe.sem_inc(t_done, 1)
            tiles_ahead(pe, logits, product)

        @block.scalar
        def _(act):
            def query(i):
                act.wait_ge(l_done, i + 1)
                nc.scalar.activation(qs[:, :, :], qT[:, :, bass.ds(i * P, P)], ACT.Copy).then_inc(q_ready, 1)

            def exps(i, u):
                if not (type(i) is int and i == T - 1):
                    query(i + 1)
                act.wait_ge(max_ready, i + 1)
                act.wait_ge(t_done, i * NG + 1)
                act.wait_ge(r_ready, i + 1)
                nc.scalar.activation(A[:, :], s[:, :], ACT.Exp, bias=nmax, accum_out=Z).then_inc(e_ready, 1)

            def moves(i, u):
                act.wait_ge(m_done, i + 1)
                for g in range(NG):
                    act.wait_ge(t_done, i * NG + (g + 2))
                    nc.scalar.activation(AT[:, g * G:(g + 1) * G, :],
                                         core.bank(4 + g % 2).rearrange("p (c n) -> p c n", c=G), ACT.Copy) \
                        .then_inc(t_moved, 1)

            act.sem_inc(t_moved, 2)
            query(0)
            exps(0, 0)
            with act.Fori(0, T - 2) as i:
                moves(i, 0)
                exps(i + 1, 0)
            moves(T - 2, 0)
            exps(T - 1, 0)
            moves(T - 1, 0)

        @block.vector
        def _(dve):
            PER = 4

            def mask(i, u):
                link = Chain(dve, vec, i * PER)
                dve.wait_ge(l_done, i + 2)
                dve.wait_ge(e_ready, i) if not (type(i) is int and i == 0) else None
                dve.wait_ge(adj_in[u], (i - u) * 8 + 16)
                nc.vector.scalar_tensor_tensor(s[:, :], lbank, SCALE, adj[:, u], ALU.mult, ALU.mult).then_inc(l_read, 1)
                dve.wait_ge(l_read, i + 2)
                link(nc.vector.tensor_scalar(b[:, :], s[:, :], 0.0, NOTHING, ALU.is_equal, ALU.mult))
                link(nc.vector.tensor_tensor(s[:, :], s[:, :], b[:, :], ALU.add))
                link(nc.vector.tensor_reduce(mx, s[:, :], AX.X, ALU.max))
                link(nc.vector.tensor_scalar(nmax, mx, -1.0, None, ALU.mult))
                dve.sem_inc(max_ready, 1)

            def out(i, u):
                dve.wait_ge(e_ready, i + 1)
                nc.vector.reciprocal(rZ, Z).then_inc(r_ready, 1)
                dve.wait_ge(r_ready, i + 2)
                dve.wait_ge(m_done, i + 2)
                nc.vector.tensor_scalar(o[:, :], mbank, rZ, 0.0, ALU.mult, ALU.max).then_inc(o_chain, 1)
                dve.wait_ge(o_chain, i + 1)
                dve.wait_ge(x_in[u], (i - u) * 8 + 16)
                nc.vector.tensor_tensor(xt[:, u], xt[:, u], o[:, :], ALU.add).then_inc(o_ready, 1)

            o_chain = sem("o_chain")
            dve.sem_inc(l_read, 1)
            dve.sem_inc(r_ready, 1)
            dve.sem_inc(o_ready, 2)
            mask(0, 0)
            with dve.Fori(0, T // 2 - 1) as p:
                mask(p * 2 + 1, 1)
                out(p * 2, 0)
                mask(p * 2 + 2, 0)
                out(p * 2 + 1, 1)
            mask(T - 1, 1)
            out(T - 2, 0)
            out(T - 1, 1)


def mlp_out(core, m, hid, x_dram, w, b, out_dram):
    nc = core.nc
    sem = lambda n: core.sem(f"mlp_{n}")
    X = core.take(T * D, m.ring).rearrange("p (t d) -> p t d", t=T)
    hs = core.take(2 * D).rearrange("p (u d) -> p u d", u=2)
    hT = core.take(2 * D).rearrange("p (u k n) -> p u k n", u=2, k=KD)
    D1, D2, D3 = D // 2, D // 4, D // 2
    W1 = core.take(KD * D1, m.w).rearrange("p (k d) -> p k d", k=KD)
    W2 = core.take(D1 // P * D2).rearrange("p (k d) -> p k d", k=D1 // P)
    W3 = core.take(D2 // P * D3).rearrange("p (k d) -> p k d", k=D2 // P)
    W4 = core.take(D3 // P * D).rearrange("p (k d) -> p k d", k=D3 // P)
    b4 = core.take(D)
    b1, b2, b3 = core.take(D1 // P), core.take(D2 // P), core.take(D3 // P)
    lo, ex, up = (core.take(2 * D, m.big_c + 2 * D * n).rearrange("p (u d) -> p u d", u=2) for n in range(3))
    o1 = core.take(2 * D1).rearrange("p (u k n) -> p u k n", u=2, k=D1 // P)
    o2 = core.take(2 * D2).rearrange("p (u k n) -> p u k n", u=2, k=D2 // P)
    o3 = core.take(2 * D3).rearrange("p (u k n) -> p u k n", u=2, k=D3 // P)
    loaded = sem("loaded")
    lo_ready, ex_ready, h_ready, t_done, ht_ready, o_ready, stored, vec = (sem(n) for n in (
        "lo", "exp", "h", "turned", "hT", "out", "stored", "v_chain"))
    mm = [sem(f"product{n}") for n in range(4)]
    moved = [sem(f"layer{n}") for n in range(3)]
    biased = sem("biased")
    with nc.Block() as block:
        @block.sync
        def _(sp):
            for dst, src in [(W1, w[0]), (W2, w[1]), (W3, w[2]), (W4, w[3])]:
                sp.dma_start(dst[:, :, :], src).then_inc(loaded, 16)
            for dst, src in [(b1, b[0]), (b2, b[1]), (b3, b[2]), (b4, b[3])]:
                sp.dma_start(dst[:, :], src).then_inc(loaded, 16)
            sp.dma_start(X[:, :, :], x_dram.rearrange("t p d -> p t d")).then_inc(loaded, 16)
            with sp.Fori(0, T) as t:
                sp.wait_ge(o_ready, t + 3)
                sp.dma_start(rows(out_dram, t), tile(X, t)).then_inc(stored, 16)
            sp.wait_ge(stored, 16 * T)

        @block.vector
        def _(dve):
            dve.sem_inc(ht_ready, 2)
            dve.sem_inc(h_ready, 2)
            dve.sem_inc(o_ready, 2)
            dve.wait_ge(loaded, 16 * 9)
            with dve.Fori(0, T // 2) as p:
                for u in range(2):
                    dve.wait_ge(ex_ready, p * 2 + (u + 1))
                    nc.vector.tensor_scalar_min(lo[:, u], tile(hid, p * 2 + u), 0.0).then_inc(lo_ready, 1)
                for u in range(2):
                    dve.wait_ge(ex_ready, p * 2 + (u + 3))
                    dve.wait_ge(t_done, p * 2 + (u + 1))
                    nc.vector.scalar_tensor_tensor(up[:, u], tile(hid, p * 2 + u), 0.0, ex[:, u], ALU.max, ALU.add) \
                        .then_inc(vec, 1)
                    dve.wait_ge(vec, p * 2 + (u + 1))
                    nc.vector.tensor_scalar(hs[:, u], up[:, u], -1.0, None, ALU.add).then_inc(h_ready, 1)
                for u in range(2):
                    dve.wait_ge(t_done, p * 2 + (u + 3))
                    dve.wait_ge(mm[0], p * 2 + (u + 1))
                    nc.vector.tensor_copy(hT[:, u], core.bank(u).rearrange("p (k n) -> p k n", k=KD)) \
                        .then_inc(ht_ready, 1)
                for u in range(2):
                    x = tile(X, p * 2 + u)
                    nc.vector.tensor_tensor(x, x, b4[:, :], ALU.add).then_inc(biased, 1)
                    dve.wait_ge(biased, p * 2 + (u + 1))
                    dve.wait_ge(mm[3], p * 2 + (u + 3))
                    nc.vector.tensor_tensor(x, core.bank(6 + u), x, ALU.add).then_inc(o_ready, 1)

        @block.scalar
        def _(act):
            act.sem_inc(ex_ready, 2)
            for n in range(3):
                act.sem_inc(moved[n], 2)
            act.wait_ge(loaded, 16 * 9)
            with act.Fori(0, T // 2) as p:
                for u in range(2):
                    act.wait_ge(lo_ready, p * 2 + (u + 1))
                    act.wait_ge(h_ready, p * 2 + (u + 1))
                    nc.scalar.activation(ex[:, u], lo[:, u], ACT.Exp).then_inc(ex_ready, 1)
                for n, (o, bias) in enumerate(((o1, b1), (o2, b2), (o3, b3))):
                    for u in range(2):
                        act.wait_ge(mm[n], p * 2 + (u + 3))
                        act.wait_ge(mm[n + 1], p * 2 + (u + 1))
                        for c in range(o.shape[2]):
                            last = nc.scalar.activation(o[:, u, c], core.bank(2 + u + (2 if n == 1 else 0))[:, c * P:(c + 1) * P],
                                                        ACT.Relu, bias=bias[:, c:c + 1])
                        last.then_inc(moved[n], 1)

        @block.tensor
        def _(pe):
            pe.sem_inc(t_done, 2)
            for n in range(4):
                pe.sem_inc(mm[n], 2)
            pe.wait_ge(loaded, 16 * 9)
            with pe.Fori(0, T // 2) as p:
                for u in range(2):
                    pe.wait_ge(h_ready, p * 2 + (u + 3))
                    pe.wait_ge(ht_ready, p * 2 + (u + 1))
                    for k in range(KD):
                        last = nc.tensor.transpose(core.bank(u)[:, k * P:(k + 1) * P],
                                                   hs[:, u, k * P:(k + 1) * P], m.ident[:, :])
                    last.then_inc(t_done, 1)
                for u in range(2):
                    pe.wait_ge(ht_ready, p * 2 + (u + 3))
                    pe.wait_ge(moved[2], p * 2 + (u + 1))
                    for c in range(D1 // P):
                        last = accumulate(nc, core.bank(2 + u)[:, c * P:(c + 1) * P],
                                          [(W1[:, k, c * P:(c + 1) * P], hT[:, u, k]) for k in range(KD)])
                    last.then_inc(mm[0], 1)
                for u in range(2):
                    pe.wait_ge(moved[0], p * 2 + (u + 3))
                    accumulate(nc, core.bank(4 + u)[:, 0:P], [(W2[:, k], o1[:, u, k]) for k in range(D1 // P)]) \
                        .then_inc(mm[1], 1)
                for u in range(2):
                    pe.wait_ge(moved[1], p * 2 + (u + 3))
                    for c in range(D3 // P):
                        last = accumulate(nc, core.bank(2 + u)[:, c * P:(c + 1) * P],
                                          [(W3[:, k, c * P:(c + 1) * P], o2[:, u, k]) for k in range(D2 // P)])
                    last.then_inc(mm[2], 1)
                for u in range(2):
                    pe.wait_ge(moved[2], p * 2 + (u + 3))
                    pe.wait_ge(o_ready, p * 2 + (u + 1))
                    accumulate(nc, core.bank(6 + u), [(o3[:, u, k], W4[:, k]) for k in range(D3 // P)]).then_inc(mm[3], 1)


def graph_layers_kernel(nc, io):
    with ExitStack() as ctx:
        core = Core(nc, ctx)
        m = layout(core)
        m.adj_loaded, m.adj_loads = ctx.enter_context(nc.semaphore("adjacency_loaded")), 0
        dram = lambda name, shape=(T, P, D): nc.dram_tensor(name, list(shape), F32, kind="Internal").ap()
        x1, x2, x3 = dram("x1"), dram("x2"), dram("x3")
        y0, y1, xa1, xf1, xa2, xf2 = (dram(n) for n in ("y0", "y1", "xa1", "xf1", "xa2", "xf2"))
        tiles = lambda a: a.rearrange("(t p) d -> t p d", p=P)
        chunks = lambda a: a.rearrange("(k p) d -> p k d", p=P)
        adj, adjT = tiles(io["adj"]), tiles(io["adjT"])
        with core.layer():
            setup(core, m)
            hid = graph_attention(core, m, "gat0", 16, tiles(io["x"]), adjT, chunks(io["L0_W"]),
                                  io["L0_a1"], io["L0_a2"], dram("c0", (16, N)), True)
            mix_out(core, m, "mix0", hid, tiles(io["x"]), chunks(io["L0_W_out"]), io["L0_b_out"], x1)
        with core.layer():
            XA, KQ, W3, W12 = nucleus_front(core, m, x1, io["L1_W1T"], io["L1_W2"], chunks(io["L1_W3"]), y0)
            nucleus_step(core, m, "n0", XA, XA, KQ, adjT, xa1, xf1)
            XA, XF, KQ, _ = nucleus_sum(core, m, "s0", xa1, xf1, y0, chunks(io["L1_U1_0"]), chunks(io["L1_U2_0"]),
                                        W3, W12, y1)
            nucleus_step(core, m, "n1", XA, XF, KQ, adjT, xa2, xf2)
            _, _, _, Y = nucleus_sum(core, m, "s1", xa2, xf2, y1, chunks(io["L1_U1_1"]), chunks(io["L1_U2_1"]),
                                     W3, W12, None)
            nucleus_out(core, m, Y, x1, io["L1_gamma"], io["L1_beta"], x2)
        with core.layer():
            dot_attention(core, m, x2, adj, [chunks(io[f"L2_W{n}T"]) for n in "qkv"], [io[f"L2_b{n}"] for n in "qkv"], x3)
        with core.layer():
            hid = graph_attention(core, m, "gat3", 8, x3, adjT, chunks(io["L3_W"]), io["L3_a1"], io["L3_a2"],
                                  dram("c3", (8, N)), False)
            mlp_out(core, m, hid, x3, [chunks(io[f"L3_W{n}T"]) for n in range(1, 5)],
                    [io[f"L3_b{n}"] for n in range(1, 5)], tiles(io["out"]))


def kernel(**inputs):
    import numpy as np
    import concourse.bacc as bacc
    from concourse.bass_utils import run_bass_kernel_spmd

    a = {k: np.asarray(v) for k, v in inputs.items()}
    wide = lambda v: np.ascontiguousarray(np.broadcast_to(v.reshape(1, -1), (P, v.size)))
    column = lambda v: np.ascontiguousarray(v.reshape(-1, P).T)
    arrays = {
        "x": a["x"], "adj": a["adj"], "adjT": a["adj"].T,
        "L0_W": a["L0_gnn_W_seq"], "L0_a1": wide(np.tile(a["L0_gnn_a1"], 16)), "L0_a2": wide(np.tile(a["L0_gnn_a2"], 16)),
        "L0_W_out": a["L0_gnn_W_out"], "L0_b_out": wide(a["L0_gnn_b_out"]),
        "L1_W1T": a["L1_gnn_W1"].T, "L1_W2": a["L1_gnn_W2"], "L1_W3": a["L1_gnn_W3"],
        **{f"L1_U{n}": a[f"L1_gnn_U{n}"] for n in ("1_0", "1_1", "2_0", "2_1")},
        "L1_gamma": wide(a["L1_gnn_gamma"]), "L1_beta": wide(a["L1_gnn_beta"]),
        **{f"L2_W{n}T": a[f"L2_gnn_W_{n}"].T for n in "qkv"},
        "L2_bq": column(a["L2_gnn_b_q"]), "L2_bk": column(a["L2_gnn_b_k"]), "L2_bv": wide(a["L2_gnn_b_v"]),
        "L3_W": a["L3_gnn_W"].transpose(1, 0, 2).reshape(D, D),
        "L3_a1": wide(a["L3_gnn_a1"]), "L3_a2": wide(a["L3_gnn_a2"]),
        **{f"L3_W{n}T": a[f"L3_gnn_W{n}"].T for n in range(1, 5)},
        **{f"L3_b{n}": column(a[f"L3_gnn_b{n}"]) for n in range(1, 4)}, "L3_b4": wide(a["L3_gnn_b4"]),
    }
    nc = bacc.Bacc("TRN2", target_bir_lowering=False, num_devices=1)
    io = {}
    for name, v in arrays.items():
        arrays[name] = v = np.ascontiguousarray(v)
        io[name] = nc.dram_tensor(name, v.shape, mybir.dt.from_np(v.dtype), kind="ExternalInput").ap()
    io["out"] = nc.dram_tensor("out", (N, D), F32, kind="ExternalOutput").ap()
    graph_layers_kernel(nc, io)
    r = run_bass_kernel_spmd(nc, [arrays], core_ids=[0])
    return r.results[0]["out"]
```

```python
import concourse.bass as bass
from concourse import mybir
import math
from contextlib import ExitStack, contextmanager

F32 = mybir.dt.float32
BF16 = mybir.dt.bfloat16
ALU = mybir.AluOpType
ACT = mybir.ActivationFunctionType
AX = mybir.AxisListType
RMAX = bass.bass_isa.ReduceOp.max

P = 128
N = 2048
D = 512
T = N // P
KD = D // P
BANK = 512
LN_EPS = 1e-5
TOP_EXPONENT = 76.0
SLOPE = 0.2
QUARTERS = 4
TOP_P = 0.9
DEPTH = 9.94
HALVINGS = 16
V_COLS = 1344
S_COLS = N - V_COLS
NOTHING = -10000.0
W2N = 64


class Chain:

    def __init__(self, eng, sem, base=0):
        self.eng, self.sem, self.base, self.k = eng, sem, base, 0

    def __call__(self, ins):
        ins.then_inc(self.sem, 1)
        self.k += 1
        self.eng.wait_ge(self.sem, self.base + self.k)


class Core:

    WORDS = 53000

    def __init__(self, nc, ctx):
        self.nc, self.ctx = nc, ctx
        self.sb = ctx.enter_context(nc.sbuf_tensor("arena", [P, self.WORDS], F32))
        self.ps = ctx.enter_context(nc.psum_tensor("banks", [P, 8 * BANK], F32))
        self.at = 0

    def take(self, words, at=None):
        if at is not None:
            self.at = at
        a = self.at
        self.at += words
        assert self.at <= self.WORDS, self.at
        return self.sb[:, a:a + words]

    def bank(self, b, n=1):
        return self.ps[:, b * BANK:(b + n) * BANK]

    def sem(self, name):
        self.sems.append(self.stack.enter_context(self.nc.semaphore(name)))
        return self.sems[-1]

    @contextmanager
    def layer(self):
        self.sems = []
        with ExitStack() as self.stack:
            yield
            with self.nc.Block() as block:
                @block.sync
                def _(sp):
                    for s in self.sems:
                        sp.sem_clear(s)


def tile(ap, t):
    return ap[:, bass.ds(t, 1), :].rearrange("p a b -> p (a b)")


def rows(dram, t):
    return dram[bass.ds(t, 1), :, :].rearrange("a p b -> (a p) b")


def cols(ap, t, w):
    return ap[:, bass.ds(t * w, w)]


def tiles_ahead(eng, before, at):
    before(0, 0)
    with eng.Fori(0, T // 2 - 1) as p:
        before(p * 2 + 1, 1)
        at(p * 2, 0)
        before(p * 2 + 2, 0)
        at(p * 2 + 1, 1)
    before(T - 1, 1)
    at(T - 2, 0)
    at(T - 1, 1)


def one_further(step):
    return lambda i, u: None if type(i) is int and i == T - 1 else step(i + 1, 1 - u)


def quarters_ahead(eng, before_quarter, before, at):
    TC = T // QUARTERS
    before(0, 0)
    for c in range(QUARTERS):
        before_quarter(c)
        last = c == QUARTERS - 1
        with eng.Fori(0, TC // 2 - last) as p:
            t = p * 2 + c * TC
            before(t + 1, 1)
            at(t, 0)
            before(t + 2, 0)
            at(t + 1, 1)
    before(T - 1, 1)
    at(T - 2, 0)
    at(T - 1, 1)


def layout(core):
    m = type("Buffers", (), {})()
    m.adj = core.take(T * N // 2, 0).bitcast(BF16).rearrange("p (t n) -> p t n", t=T)
    m.big_b = core.at
    core.take(T * D)
    m.big_c = core.at
    core.take(T * D)
    m.ring = core.at
    core.take(6 * N)
    m.w = core.at
    core.take(3456)
    m.small = core.at
    m.ident = core.take(P)
    m.rdeg = core.take(T)
    m.rstd = core.take(T)
    m.nmr = core.take(T)
    m.mv = core.take(2 * T).rearrange("p (t c) -> p t c", c=2)
    m.var = core.take(T)
    m.std = core.take(T)
    m.st = core.take(6)
    m.ones = core.take(1).bitcast(BF16)
    m.zeros = core.take(BANK // 2).bitcast(BF16)
    m.free = core.at
    return m


def setup(core, m):
    nc = core.nc
    s = core.sem("identity_ready")
    with nc.Block() as block:
        @block.gpsimd
        def _(pool):
            nc.gpsimd.memset(m.ident[:, :], 0.0).then_inc(s, 1)
            nc.gpsimd.memset(m.ones[:, :], 1.0).then_inc(s, 1)
            nc.gpsimd.memset(m.zeros[:, :], 0.0).then_inc(s, 1)
            pool.wait_ge(s, 3)
            nc.gpsimd.affine_select(out=m.ident[:, :], in_=m.ident[:, :], compare_op=ALU.not_equal, fill=1.0,
                                    base=0, pattern=[[-1, P]], channel_multiplier=1).then_inc(s, 1)


def front(core, m, tag, x_dram, weights, loads=(), project=None, evac_dve=None, evac_act=None,
          natural=None, prepare=None, pool_first=None):
    nc = core.nc
    sem = lambda n: core.sem(f"{tag}_{n}")
    X = core.take(T * D, m.ring).rearrange("p (t d) -> p t d", t=T)
    hs = core.take(2 * D).rearrange("p (u d) -> p u d", u=2)
    hT = core.take(2 * D).rearrange("p (u k n) -> p u k n", u=2, k=KD)
    x_in = [sem(f"x_loaded{c}") for c in range(QUARTERS)]
    w_in = sem("weights_loaded")
    vecs, stats, root, norm = sem("vector_chain"), sem("variance_ready"), sem("root_ready"), sem("scales_ready")
    prep = sem("weights_prepared")
    h_ready, t_done, ht_ready = sem("h_ready"), sem("transposed"), sem("hT_ready")
    mm_done, dve_out, act_out, nat_out = sem("projected"), sem("vector_moved"), sem("scalar_moved"), sem("natural_moved")
    TC = T // QUARTERS

    with nc.Block() as block:
        @block.sync
        def _(sp):
            for c in range(QUARTERS):
                sp.dma_start(X[:, c * TC:(c + 1) * TC, :],
                             x_dram[c * TC:(c + 1) * TC, :, :].rearrange("t p d -> p t d")).then_inc(x_in[c], 16)
                if c == 0:
                    for dst, src in weights:
                        sp.dma_start(dst, src).then_inc(w_in, 16)
            sp.wait_ge(w_in, 16 * len(weights))

        @block.vector
        def _(dve):
            own = Chain(dve, vecs)

            def statistics(c):
                part = slice(c * TC, (c + 1) * TC)
                dve.wait_ge(x_in[c], 16)
                for t in range(c * TC, (c + 1) * TC):
                    own(nc.vector.bn_stats(m.st[:, :], X[:, t]))
                    own(nc.vector.bn_aggr(m.mv[:, t], m.st[:, :]))
                nc.vector.tensor_scalar_add(m.var[:, part], m.mv[:, part, 1], LN_EPS).then_inc(stats, 1)
                dve.wait_ge(root, c + 1)
                own(nc.vector.reciprocal(m.rstd[:, part], m.std[:, part]))
                nc.vector.scalar_tensor_tensor(m.nmr[:, part], m.mv[:, part, 0], -1.0, m.rstd[:, part],
                                               ALU.mult, ALU.mult).then_inc(norm, 1)

            statistics(0)
            if prepare is not None:
                dve.wait_ge(w_in, 16 * len(weights))
                prepare(nc, dve, own)
                dve.sem_inc(prep, 1)
            dve.sem_inc(ht_ready, 2)
            if evac_dve is not None:
                dve.sem_inc(dve_out, 2)

            def move(i, u):
                dve.wait_ge(t_done, i + 3)
                dve.wait_ge(mm_done, i + 1)
                nc.vector.tensor_copy(hT[:, u], core.bank(u).rearrange("p (k n) -> p k n", k=KD)).then_inc(ht_ready, 1)

            def evacuate(i, u):
                if evac_dve is not None:
                    dve.wait_ge(mm_done, i + 3)
                    evac_dve(nc, i, u).then_inc(dve_out, 1)

            quarters_ahead(dve, lambda c: statistics(c + 1) if c + 1 < QUARTERS else None, move, evacuate)

        @block.scalar
        def _(act):
            def deviation(c):
                part = slice(c * TC, (c + 1) * TC)
                act.wait_ge(stats, c + 1)
                nc.scalar.activation(m.std[:, part], m.var[:, part], ACT.Sqrt).then_inc(root, 1)

            deviation(0)
            if evac_act is not None:
                act.sem_inc(act_out, 2)

            def normalise(i, u):
                act.wait_ge(t_done, i + 1)
                if natural is not None:
                    act.wait_ge(nat_out, i + 1)
                nc.scalar.activation(hs[:, u], tile(X, i), ACT.Relu, bias=cols(m.nmr, i, 1),
                                     scale=cols(m.rstd, i, 1)).then_inc(h_ready, 1)

            def evacuate(i, u):
                if evac_act is not None:
                    act.wait_ge(mm_done, i + 3)
                    evac_act(nc, i, u).then_inc(act_out, 1)

            def next_quarter(c):
                if c + 1 < QUARTERS:
                    deviation(c + 1)
                    act.wait_ge(norm, c + 2)

            act.wait_ge(norm, 1)
            normalise(0, 0)
            quarters_ahead(act, next_quarter, one_further(normalise), evacuate)

        @block.tensor
        def _(pe):
            pe.wait_ge(w_in, 16 * len(weights))
            if prepare is not None:
                pe.wait_ge(prep, 1)
            pe.sem_inc(t_done, 2)
            pe.sem_inc(mm_done, 2)

            def turn(i, u):
                pe.wait_ge(h_ready, i + 1)
                pe.wait_ge(ht_ready, i + 1)
                for k in range(KD):
                    last = nc.tensor.transpose(core.bank(u)[:, k * P:(k + 1) * P],
                                               hs[:, u, k * P:(k + 1) * P], m.ident[:, :])
                last.then_inc(t_done, 1)

            def products(i, u):
                pe.wait_ge(ht_ready, i + 3)
                if evac_dve is not None:
                    pe.wait_ge(dve_out, i + 1)
                if evac_act is not None:
                    pe.wait_ge(act_out, i + 1)
                project(nc, hT[:, u], u).then_inc(mm_done, 1)

            tiles_ahead(pe, turn, products)

        @block.gpsimd
        def _(pool):
            if pool_first is not None:
                pool_first(nc, pool)
            if natural is not None:
                pool.sem_inc(nat_out, 2)
                with pool.Fori(0, T // 2) as p:
                    for u in range(2):
                        pool.wait_ge(h_ready, p * 2 + (u + 1))
                        nc.gpsimd.tensor_copy(tile(natural, p * 2 + u), hs[:, u]).then_inc(nat_out, 1)


def accumulate(nc, out, pairs):
    last = None
    for n, (lhsT, rhs) in enumerate(pairs):
        last = nc.tensor.matmul(out, lhsT, rhs, start=(n == 0), stop=(n == len(pairs) - 1))
    return last


def graph_attention(core, m, tag, heads, x_dram, adjT, w_dram, a1_dram, a2_dram, c_dram, degree):
    nc = core.nc
    H, DH = heads, D // heads
    m.adj_loads += 1
    W = core.take(KD * D, m.w).rearrange("p (k d) -> p k d", k=KD)
    a1, a2 = core.take(D), core.take(D)
    w12 = core.take(KD * 2 * H).rearrange("p (k h) -> p k h", k=KD)
    prod = core.take(KD * D, m.big_c).rearrange("p (k d) -> p k d", k=KD)
    V = core.take(T * D, m.big_c).rearrange("p (t d) -> p t d", t=T)
    hid = core.take(T * D, m.big_b).rearrange("p (t d) -> p t d", t=T)
    s_rows = core.take(2 * N, m.big_b).rearrange("p (s n) -> p s n", s=2)
    c_rows = core.take(N)
    S = core.take(T * 2 * H, m.free).rearrange("p (t h) -> p t h", t=T)
    G, FF = (core.take(T * H).rearrange("p (t h) -> p t h", t=T) for _ in range(2))
    top, colmax, rowtop = core.take(H), core.take(H), core.take(1)
    recip = core.take(T)

    def load_adjacency(nc, pool):
        for t in range(T):
            pool.dma_start(m.adj[:, t, :], adjT[t, :, :]).then_inc(m.adj_loaded, 16)

    def prepare(nc, dve, link):
        for n, a in enumerate((a1, a2)):
            link(nc.vector.tensor_tensor(prod[:, :, :], W[:, :, :], a.unsqueeze(1).broadcast_to([P, KD, D]), ALU.mult))
            for k in range(KD):
                link(nc.vector.tensor_reduce(w12[:, k, n * H:(n + 1) * H],
                                             prod[:, k].rearrange("p (h d) -> p h d", h=H), AX.X, ALU.add))

    def project(nc, hT, u):
        v, s = core.bank(2 + u), core.bank(4 + u)
        accumulate(nc, v[:, :], [(hT[:, k], W[:, k]) for k in range(KD)])
        accumulate(nc, s[:, 0:2 * H], [(hT[:, k], w12[:, k]) for k in range(KD)])
        accumulate(nc, s[0:H, P:2 * P], [(w12[:, k, 0:H], hT[:, k]) for k in range(KD)])
        return accumulate(nc, s[0:H, 2 * P:3 * P], [(w12[:, k, H:2 * H], hT[:, k]) for k in range(KD)])

    def evac_dve(nc, t, u):
        s = core.bank(4 + u)
        nc.vector.tensor_copy(s_rows[0:H, :, bass.ds(t * P, P)], s[0:H, P:3 * P].rearrange("p (s n) -> p s n", s=2))
        return nc.vector.tensor_copy(tile(S, t), s[:, 0:2 * H])

    def evac_act(nc, t, u):
        return nc.scalar.activation(tile(V, t), core.bank(2 + u), ACT.Copy)

    front(core, m, tag, x_dram, [(W[:, :, :], w_dram), (a1[:, :], a1_dram), (a2[:, :], a2_dram)],
          project=project, evac_dve=evac_dve, evac_act=evac_act, prepare=prepare, pool_first=load_adjacency)

    sem = lambda n: core.sem(f"{tag}_{n}")
    link_s, colmax_ready, top_ready, diff_ready = sem("v_chain"), sem("colmax_ready"), sem("top_ready"), sem("diff_ready")
    row_ready, c_ready, c_stored, exp_ready = sem("row_ready"), sem("c_ready"), sem("c_stored"), sem("exp_ready")
    with nc.Block() as block:
        @block.vector
        def _(dve):
            link = Chain(dve, link_s)
            link(nc.vector.tensor_reduce(colmax[:, :], S[:, :, H:2 * H].rearrange("p t h -> p h t"), AX.X, ALU.max))
            dve.sem_inc(colmax_ready, 1)
            link(nc.vector.tensor_reduce(rowtop[0:H, :], s_rows[0:H, 1, :], AX.X, ALU.max))
            link(nc.vector.tensor_scalar(c_rows[0:H, :], s_rows[0:H, 0, :], rowtop[0:H, 0:1], 1.0 - SLOPE,
                                         ALU.add, ALU.mult))
            nc.vector.tensor_scalar_min(c_rows[0:H, :], c_rows[0:H, :], TOP_EXPONENT).then_inc(row_ready, 1)
            dve.wait_ge(top_ready, 1)
            nc.vector.tensor_tensor(S[:, :, 0:H], S[:, :, H:2 * H], top.unsqueeze(1).broadcast_to([P, T, H]),
                                    ALU.subtract).then_inc(diff_ready, 1)
            dve.wait_ge(exp_ready, 2)
            with dve.Fori(0, T) as t:
                v = tile(V, t).rearrange("p (h e) -> p h e", h=H)
                nc.vector.tensor_tensor(v, v, FF[:, bass.ds(t, 1), :].rearrange("p a h -> p (a h)").unsqueeze(2)
                                        .broadcast_to([P, H, DH]), ALU.mult)

        @block.gpsimd
        def _(pool):
            pool.wait_ge(m.adj_loaded, 16 * T * m.adj_loads)
            pool.wait_ge(colmax_ready, 1)
            nc.gpsimd.partition_all_reduce(top[:, :], colmax[:, :], P, RMAX).then_inc(top_ready, 1)

        @block.scalar
        def _(act):
            act.wait_ge(row_ready, 1)
            nc.scalar.activation(c_rows[0:H, :], c_rows[0:H, :], ACT.Exp).then_inc(c_ready, 1)
            act.wait_ge(diff_ready, 1)
            nc.scalar.activation(G[:, :, :], S[:, :, 0:H], ACT.Exp, scale=1.0 - SLOPE).then_inc(exp_ready, 1)
            act.wait_ge(exp_ready, 1)
            nc.scalar.activation(FF[:, :, :], S[:, :, 0:H], ACT.Exp, scale=SLOPE).then_inc(exp_ready, 1)

        @block.sync
        def _(sp):
            sp.wait_ge(c_ready, 1)
            sp.dma_start(c_dram[:, :], c_rows[0:H, :]).then_inc(c_stored, 16)
            sp.wait_ge(c_stored, 16)

    Q = 32
    IB = N // BANK
    nc_ = DH // Q
    nb = nc_ + 1
    cb = core.take(2 * N, m.ring).rearrange("p (u n) -> p u n", u=2)
    Wt = core.take(2 * N).rearrange("p (u n) -> p u n", u=2)
    Pt = core.take(2 * N).rearrange("p (u n) -> p u n", u=2)
    Vs = core.take(2 * (DH + Q), m.w).rearrange("p (u e) -> p u e", u=2)
    ns = core.take(nb * BANK).rearrange("p (b n) -> p b n", b=nb)
    sums = lambda par, b: core.bank(nb * par + b)
    c_in = [sem(f"c_loaded{u}") for u in range(2)]
    relu_done, prob_done, mm_done, fin_done = sem("relu_done"), sem("prob_done"), sem("head_products"), sem("head_done")
    v_ready, ns_ready, turned = sem("values_ready"), sem("sums_moved"), sem("sums_turned")
    fin_s, deg_done = sem("fin_chain"), sem("degree_done")

    def heads_in_pairs(eng, head):
        head(0, 0, False)
        with eng.Fori(0, H // 2 - 1) as p:
            head(p * 2 + 1, 1, True)
            head(p * 2 + 2, 0, True)
        head(H - 1, 1, True)

    with nc.Block() as block:
        @block.sync
        def _(sp):
            with sp.Fori(0, H // 2) as p:
                for u in range(2):
                    sp.wait_ge(relu_done, p * (2 * T) + (u * T + T))
                    sp.dma_start(cb[:, u, :], c_dram[bass.ds(p * 2 + u, 1), :].rearrange("a n -> (a n)")
                                 .partition_broadcast(P)).then_inc(c_in[u], 16)
            sp.wait_ge(c_in[0], 16 * (H // 2))
            sp.wait_ge(c_in[1], 16 * (H // 2))

        @block.gpsimd
        def _(pool):
            with pool.Fori(0, H) as h:
                with pool.Fori(0, T // 2) as q:
                    for v in range(2):
                        n = h * T + q * 2 + v
                        pool.wait_ge(mm_done, n + 1)
                        nc.gpsimd.tensor_copy(Vs[:, v, 0:DH], V[:, bass.ds(q * 2 + v, 1), bass.ds(h * DH, DH)]
                                              .rearrange("p a d -> p (a d)"))
                        nc.gpsimd.tensor_copy(Vs[:, v, DH:DH + Q], FF[:, bass.ds(q * 2 + v, 1), bass.ds(h, 1)]
                                              .rearrange("p a b -> p (a b)").broadcast_to([P, Q])).then_inc(v_ready, 1)

        @block.scalar
        def _(act):
            act.sem_inc(relu_done, 2 * T)

            def head(h, par, before):
                act.wait_ge(c_in[par], (h - par) * 8 + 16)

                def relu(jt, v):
                    act.wait_ge(prob_done, h * T + (jt + 1))
                    g = G[:, bass.ds(jt, 1), bass.ds(h, 1)].rearrange("p a b -> p (a b)")
                    nc.scalar.activation(Wt[:, v], cb[:, par], ACT.Relu, bias=-1.0, scale=g).then_inc(relu_done, 1)

                for jt in range(4):
                    relu(jt, jt % 2)
                if before:
                    move_sums(h - 1, 1 - par)
                with act.Fori(2, T // 2) as q:
                    for v in range(2):
                        relu(q * 2 + v, v)

            def move_sums(h, par):
                act.wait_ge(mm_done, h * T + (T + 2))
                act.wait_ge(turned, h + 1)
                for b in range(nb):
                    last = nc.scalar.activation(ns[:, b], sums(par, b), ACT.Copy)
                last.then_inc(ns_ready, 1)

            heads_in_pairs(act, head)
            move_sums(H - 1, 1)

        @block.vector
        def _(dve):
            dve.sem_inc(prob_done, 2)
            dve.sem_inc(fin_done, 2)

            def finish(h, par):
                dve.wait_ge(turned, h + 2)
                turned_den = sums(par, nc_).rearrange("p (n d) -> p n d", d=Q)
                nc.vector.reciprocal(recip[:, :], turned_den[:, :, 0]).then_inc(fin_s, 1)
                dve.wait_ge(fin_s, h + 1)
                for b in range(nc_):
                    out = hid[:, :, bass.ds(h * DH + b * Q, Q)].rearrange("p (i c) d -> p c i d", i=IB)
                    last = nc.vector.tensor_tensor(
                        out, sums(par, b).rearrange("p (c i d) -> p c i d", i=IB, d=Q),
                        recip.rearrange("p (c i) -> p c i", i=IB).unsqueeze(3).broadcast_to([P, IB, IB, Q]), ALU.mult)
                last.then_inc(fin_done, 1)

            def head(h, par, before):
                def prob(jt, v):
                    dve.wait_ge(relu_done, h * T + (jt + 1 + 2 * T))
                    dve.wait_ge(mm_done, h * T + (jt + 1))
                    nc.vector.scalar_tensor_tensor(Pt[:, v], Wt[:, v], 1.0, tile(m.adj, jt), ALU.add, ALU.mult) \
                        .then_inc(prob_done, 1)

                for jt in range(6):
                    prob(jt, jt % 2)
                if before:
                    finish(h - 1, 1 - par)
                with dve.Fori(3, T // 2) as q:
                    for v in range(2):
                        prob(q * 2 + v, v)

            heads_in_pairs(dve, head)
            finish(H - 1, 1)
            if degree:
                dve.wait_ge(deg_done, 1)
                link = Chain(dve, fin_s, H)
                link(nc.vector.tensor_scalar(m.rdeg[:, :], core.bank(7)[:, 0:T], 1.0, 1e-12, ALU.add, ALU.max))
                link(nc.vector.reciprocal(m.rdeg[:, :], m.rdeg[:, :]))

        @block.tensor
        def _(pe):
            pe.sem_inc(mm_done, 2)
            pe.sem_inc(turned, 1)

            def turn(h, par):
                pe.wait_ge(ns_ready, h + 1)
                for b in range(nb):
                    for c in range(IB):
                        last = nc.tensor.transpose(sums(par, b)[:, c * P:(c + 1) * P], ns[:, b, c * P:(c + 1) * P],
                                                   m.ident[:, :])
                last.then_inc(turned, 1)

            def head(h, par, before):
                def products(jt, v):
                    pe.wait_ge(prob_done, h * T + (jt + 3))
                    pe.wait_ge(v_ready, h * T + (jt + 1))
                    for b in range(nb):
                        for i in range(IB):
                            last = nc.tensor.matmul(sums(par, b)[i * Q:(i + 1) * Q, :], Vs[:, v, b * Q:(b + 1) * Q],
                                                    Pt[:, v, i * BANK:(i + 1) * BANK], start=False, stop=False,
                                                    skip_group_check=True)
                    last.then_inc(mm_done, 1)

                pe.wait_ge(fin_done, h + 1)
                for b in range(nb):
                    nc.tensor.matmul(sums(par, b), m.zeros[:, 0:P], m.zeros[:, :], start=True, stop=False,
                                     skip_group_check=True)
                for jt in range(4):
                    products(jt, jt % 2)
                if before:
                    turn(h - 1, 1 - par)
                with pe.Fori(2, T // 2) as q:
                    for v in range(2):
                        products(q * 2 + v, v)

            heads_in_pairs(pe, head)
            turn(H - 1, 1)
            if degree:
                for it in range(T):
                    last = accumulate(nc, core.bank(7)[:, it:it + 1],
                                      [(m.adj[:, jt, it * P:(it + 1) * P], m.ones[:, 0:1]) for jt in range(T)])
                last.then_inc(deg_done, 1)
    return hid


def mix_out(core, m, tag, hid, x_dram, w_dram, b_dram, y_dram):
    nc = core.nc
    sem = lambda n: core.sem(f"{tag}_{n}")
    X = core.take(T * D, m.ring).rearrange("p (t d) -> p t d", t=T)
    hs = core.take(2 * D).rearrange("p (u d) -> p u d", u=2)
    hT = core.take(2 * D).rearrange("p (u k n) -> p u k n", u=2, k=KD)
    W = core.take(KD * D, m.w).rearrange("p (k d) -> p k d", k=KD)
    b = core.take(D)
    yb, lo, ex, o = (core.take(2 * D, m.big_c + 2 * D * n).rearrange("p (u d) -> p u d", u=2) for n in range(4))
    w_in, x_in = sem("weights_loaded"), sem("x_loaded")
    h_ready, t_done, ht_ready, mm_done = sem("h_ready"), sem("transposed"), sem("hT_ready"), sem("projected")
    vec, lo_ready, ex_ready, o_ready, stored = sem("v_chain"), sem("lo_ready"), sem("exp_ready"), sem("o_ready"), sem("stored")
    biased = sem("biased")
    with nc.Block() as block:
        @block.sync
        def _(sp):
            sp.dma_start(W[:, :, :], w_dram).then_inc(w_in, 16)
            sp.dma_start(b[:, :], b_dram).then_inc(w_in, 16)
            sp.dma_start(X[:, :, :], x_dram.rearrange("t p d -> p t d")).then_inc(x_in, 16)
            with sp.Fori(0, T) as t:
                sp.wait_ge(o_ready, t + 1)
                sp.dma_start(rows(y_dram, t), tile(X, t)).then_inc(stored, 16)
            sp.wait_ge(stored, 16 * T)

        @block.scalar
        def _(act):
            def copy(i, u):
                act.wait_ge(t_done, i + 1)
                nc.scalar.activation(hs[:, u], tile(hid, i), ACT.Copy).then_inc(h_ready, 1)

            def exp(i, u):
                act.wait_ge(lo_ready, i + 1)
                nc.scalar.activation(ex[:, u], lo[:, u], ACT.Exp).then_inc(ex_ready, 1)

            copy(0, 0)
            tiles_ahead(act, one_further(copy), exp)

        @block.tensor
        def _(pe):
            def turn(i, u):
                pe.wait_ge(h_ready, i + 1)
                pe.wait_ge(ht_ready, i + 1)
                for k in range(KD):
                    last = nc.tensor.transpose(core.bank(u)[:, k * P:(k + 1) * P],
                                               hs[:, u, k * P:(k + 1) * P], m.ident[:, :])
                last.then_inc(t_done, 1)

            def product(i, u):
                pe.wait_ge(ht_ready, i + 3)
                pe.wait_ge(biased, i + 1)
                accumulate(nc, core.bank(2 + u), [(hT[:, u, k], W[:, k]) for k in range(KD)]).then_inc(mm_done, 1)

            pe.sem_inc(t_done, 2)
            pe.sem_inc(mm_done, 2)
            pe.wait_ge(w_in, 32)
            tiles_ahead(pe, turn, product)

        @block.vector
        def _(dve):
            def move(i, u):
                dve.wait_ge(t_done, i + 3)
                dve.wait_ge(mm_done, i + 1)
                nc.vector.tensor_copy(hT[:, u], core.bank(u).rearrange("p (k n) -> p k n", k=KD)) \
                    .then_inc(ht_ready, 1)

            def elu(i, u):
                dve.wait_ge(mm_done, i + 3)
                nc.vector.tensor_tensor(yb[:, u], core.bank(2 + u), b[:, :], ALU.add).then_inc(biased, 1)
                dve.wait_ge(biased, i + 3)
                nc.vector.tensor_scalar_min(lo[:, u], yb[:, u], 0.0).then_inc(lo_ready, 1)
                dve.wait_ge(ex_ready, i + 1)
                nc.vector.scalar_tensor_tensor(o[:, u], yb[:, u], 0.0, ex[:, u], ALU.max, ALU.add).then_inc(vec, 1)
                dve.wait_ge(vec, i + 1)
                nc.vector.scalar_tensor_tensor(tile(X, i), o[:, u], -1.0, tile(X, i), ALU.add, ALU.add) \
                    .then_inc(o_ready, 1)

            dve.sem_inc(ht_ready, 2)
            dve.sem_inc(biased, 2)
            dve.wait_ge(w_in, 32)
            dve.wait_ge(x_in, 16)
            tiles_ahead(dve, move, elu)


def nucleus_front(core, m, x_dram, w1t_dram, w2_dram, w3_dram, h_dram):
    nc = core.nc
    A = W2N
    W3 = core.take(KD * A, m.w).rearrange("p (k a) -> p k a", k=KD)
    W12 = core.take(KD * A).rearrange("p (k a) -> p k a", k=KD)
    W1T, W2 = core.take(D), core.take(A)
    XA = core.take(T * D, m.big_b).rearrange("p (t d) -> p t d", t=T)
    KQ = core.take(2 * N, T * D).rearrange("p (s n) -> p s n", s=2)
    folded, stored = core.sem("nf_folded"), core.sem("nf_stored")

    def project(nc, hT, u):
        accumulate(nc, core.bank(2 + u)[0:A, 0:P], [(W3[:, k], hT[:, k]) for k in range(KD)])
        return accumulate(nc, core.bank(2 + u)[0:A, P:2 * P], [(W12[:, k], hT[:, k]) for k in range(KD)])

    def evac_dve(nc, t, u):
        return nc.vector.tensor_copy(KQ[0:A, :, bass.ds(t * P, P)],
                                     core.bank(2 + u)[0:A, 0:2 * P].rearrange("p (s n) -> p s n", s=2))

    fold_in = core.sem("nf_fold_loaded")
    with nc.Block() as block:
        @block.sync
        def _(sp):
            sp.dma_start(W1T[0:A, :], w1t_dram).then_inc(fold_in, 16)
            sp.dma_start(W2[0:A, :], w2_dram).then_inc(fold_in, 16)

        @block.tensor
        def _(pe):
            pe.wait_ge(fold_in, 32)
            for k in range(KD):
                last = nc.tensor.matmul(core.bank(6)[:, k * A:(k + 1) * A], W1T[0:A, k * P:(k + 1) * P], W2[0:A, :],
                                        start=True, stop=True)
            last.then_inc(folded, 1)

        @block.vector
        def _(dve):
            dve.wait_ge(folded, 1)
            nc.vector.tensor_copy(W12[:, :, :], core.bank(6)[:, 0:KD * A].rearrange("p (k a) -> p k a", k=KD))

    front(core, m, "nf", x_dram, [(W3[:, :, :], w3_dram)], project=project, evac_dve=evac_dve, natural=XA)
    with nc.Block() as block:
        @block.sync
        def _(sp):
            sp.dma_start(h_dram.rearrange("t p d -> p t d"), XA[:, :, :]).then_inc(stored, 16)
    return XA, KQ, W3, W12, stored


def nucleus_step(core, m, tag, XA, XF, KQ, adjT, xa_out, xf_out):
    nc = core.nc
    sem = lambda n: core.sem(f"{tag}_{n}")
    E = core.take(2 * N, m.ring).rearrange("p (u n) -> p u n", u=2)
    masked = core.take(V_COLS).bitcast(BF16).rearrange("p (u n) -> p u n", u=2)
    B = core.take(N)
    A = core.take(N)
    AT = core.take(N).rearrange("p (t n) -> p t n", t=T)
    C = core.take(N + 4, m.big_c)
    adj = core.take(N).rearrange("p (t n) -> p t n", t=T)
    xas, xfs = core.take(D), core.take(D)
    ramp = core.take(S_COLS).bitcast(BF16).rearrange("p (u n) -> p u n", u=2)
    sign = core.take(S_COLS).bitcast(BF16).rearrange("p (u n) -> p u n", u=2)
    qs = core.take(P, m.free)
    small = core.take(32)
    mx, nmax, Z1, Z2, nmid, goal, mid, got, r, s, q, above, rS = (small[:, 2 * n:2 * n + 2] for n in range(13))
    aim, low, high, all_, left, S = (small[:, n:n + 1] for n in range(26, 32))
    q_ready, l_done, max_done, nmax_ready, e_ready = (sem(n) for n in ("q", "logits", "max", "minus_max", "exp"))
    adj_in, r_done, a_ready, t_done, t_moved = (sem(n) for n in ("adj", "r_product", "nucleus", "turned", "turned_moved"))
    m_done, s_done, xa_ready, xa_stored, rs_ready = (sem(n) for n in ("a_product", "searched", "xa", "xa_stored", "a_sum"))
    xf_moved, xf_chain, xf_ready, xf_stored, vec = (sem(n) for n in ("xf_moved", "xf_sum", "xf", "xf_stored", "v_chain"))
    mid_ready, nmid_ready, got_ready, acc_ready, ends_ready, gp = (sem(n) for n in (
        "mid", "minus_mid", "v_sum", "s_sums", "interval", "g_chain"))
    G = 4
    NG = T // G
    lbank, rbank, mbank = core.bank(0, 4), core.bank(7), core.bank(6)
    HALF = HALVINGS // 2
    TURNS = {True: (11, 12, 13, 14), False: (4, 5, 6, 7)}
    ratio = lambda h: math.exp(DEPTH / 2 ** (h + 2))
    SLACK = 4e-6
    first_mid = lambda i: i * (2 * HALF + 1) + HALF + 2
    first_sum = lambda i: i * (2 * HALF) + HALF

    def rounds(eng, body):
        for i in range(2):
            body(i, i)
        with eng.Fori(0, (T - 4) // 2) as p:
            body(p * 2 + 2, 0)
            body(p * 2 + 3, 1)
        for i in range(T - 2, T):
            body(i, i % 2)

    fixed = lambda i, n: type(i) is int and i == n
    beyond = lambda i, n: type(i) is int and i >= n

    def halvings(i, u):
        for h in range(HALF):
            if fixed(i, T - 1):
                yield u, HALF + h, h
            else:
                yield u, HALF + h, 2 * h
                yield 1 - u, h, 2 * h + 1

    def halving_mid(i, n):
        return first_mid(i) + (n if fixed(i, T - 1) else n - 1)

    with nc.Block() as block:
        @block.sync
        def _(sp):
            def load(i):
                sp.wait_ge(r_done, i + 1)
                sp.dma_start(adj[:, :, :], adjT[:, :, bass.ds(i * P, P)].rearrange("t p n -> p t n")) \
                    .then_inc(adj_in, 16)

            def store_xf(i):
                sp.wait_ge(xf_ready, i + 1)
                sp.dma_start(rows(xf_out, i), xfs[:, :]).then_inc(xf_stored, 16)

            def store_xa(i):
                sp.wait_ge(xa_ready, i + 2)
                sp.dma_start(rows(xa_out, i), xas[:, :]).then_inc(xa_stored, 16)

            def body(i, u):
                if not fixed(i, 0) and not fixed(i, 1):
                    store_xa(i - 2)
                if not fixed(i, T - 1):
                    load(i + 1)
                if not fixed(i, 0):
                    store_xf(i - 1)

            sp.sem_inc(xf_stored, 16)
            sp.sem_inc(xa_stored, 16)
            load(0)
            rounds(sp, body)
            store_xf(T - 1)
            store_xa(T - 2)
            store_xa(T - 1)
            sp.wait_ge(xf_stored, 16 * (T + 1))
            sp.wait_ge(xa_stored, 16 * (T + 1))

        @block.tensor
        def _(pe):
            def logits(i):
                pe.wait_ge(q_ready, i + 1)
                if not fixed(i, 0):
                    pe.wait_ge(e_ready, i * 2)
                for c in range(N // BANK):
                    last = nc.tensor.matmul(core.bank(c), qs[0:W2N, :], KQ[0:W2N, 0, c * BANK:(c + 1) * BANK],
                                            start=True, stop=True)
                last.then_inc(l_done, 1)

            def r_product(i):
                pe.wait_ge(adj_in, i * 16 + 16)
                pe.wait_ge(xf_moved, i + 1)
                accumulate(nc, rbank, [(adj[:, jt], XF[:, jt]) for jt in range(T)]).then_inc(r_done, 1)

            def turn(i):
                pe.wait_ge(a_ready, i + 1)
                for g in range(NG):
                    pe.wait_ge(t_moved, i * NG + (g + 1))
                    for c in range(G):
                        last = nc.tensor.transpose(core.bank(4 + g % 2)[:, c * P:(c + 1) * P],
                                                   A[:, (g * G + c) * P:(g * G + c + 1) * P], m.ident[:, :])
                    last.then_inc(t_done, 1)

            def a_product(i):
                pe.wait_ge(t_moved, i * NG + (NG + 2))
                pe.wait_ge(xa_ready, i + 1)
                accumulate(nc, mbank, [(AT[:, jt], XA[:, jt]) for jt in range(T)]).then_inc(m_done, 1)

            def body(i, u):
                if not beyond(i, T - 2):
                    logits(i + 2)
                r_product(i)
                if not fixed(i, 0):
                    turn(i - 1)
                    a_product(i - 1)

            pe.sem_inc(l_done, 1)
            pe.sem_inc(r_done, 1)
            pe.sem_inc(m_done, 1)
            pe.sem_inc(t_done, 1)
            logits(0)
            logits(1)
            rounds(pe, body)
            turn(T - 1)
            a_product(T - 1)

        @block.scalar
        def _(act):
            def query(i):
                act.wait_ge(l_done, i + 1)
                nc.scalar.activation(qs[0:W2N, :], KQ[0:W2N, 1, bass.ds(i * P, P)], ACT.Copy).then_inc(q_ready, 1)

            def exps(i, u):
                act.wait_ge(s_done, i + 1)
                act.wait_ge(nmax_ready, i + 1)
                for part, Z in ((slice(0, V_COLS), Z1), (slice(V_COLS, N), Z2)):
                    nc.scalar.activation(E[:, u, part], lbank[:, part], ACT.Exp, bias=nmax[:, u:u + 1],
                                         accum_out=Z[:, u:u + 1]).then_inc(e_ready, 1)

            def sums(u, mids):
                act.wait_ge(nmid_ready, mids)
                for func, out, total in ((ACT.Relu, ramp, r), (ACT.Sign, sign, s)):
                    nc.scalar.activation(out[:, u, :], E[:, u, V_COLS:N], func, bias=nmid[:, u:u + 1],
                                         accum_out=total[:, u:u + 1]).then_inc(acc_ready, 1)

            def move_xf(i):
                act.wait_ge(r_done, i + 2)
                act.wait_ge(xf_stored, i * 16 + 16)
                nc.scalar.activation(xfs[:, :], rbank, ACT.Copy).then_inc(xf_moved, 1)

            def move_turned(i, g):
                act.wait_ge(m_done, i + 1)
                act.wait_ge(t_done, i * NG + (g + 2))
                nc.scalar.activation(AT[:, g * G:(g + 1) * G, :],
                                     core.bank(4 + g % 2).rearrange("p (c n) -> p c n", c=G), ACT.Copy) \
                    .then_inc(t_moved, 1)

            def move_xa(i, u):
                act.wait_ge(m_done, i + 2)
                act.wait_ge(rs_ready, i + 1)
                act.wait_ge(xa_stored, i * 16 + 16)
                nc.scalar.activation(xas[:, :], mbank, ACT.Copy, scale=rS[:, u:u + 1]).then_inc(xa_ready, 1)

            def body(i, u):
                if not beyond(i, T - 2):
                    query(i + 2)
                many = not fixed(i, T - 1)
                for slot, h, n in halvings(i, u):
                    sums(slot, halving_mid(i, n))
                    if not fixed(i, 0) and n in TURNS[many]:
                        move_turned(i - 1, TURNS[many].index(n))
                    if n == 1 and not fixed(i, 0):
                        move_xf(i - 1)
                    if n == 5 and not fixed(i, 0) and not fixed(i, 1):
                        move_xa(i - 2, u)
                if not beyond(i, T - 2):
                    exps(i + 2, u)

            act.sem_inc(t_moved, 2)
            act.sem_inc(xf_moved, 1)
            act.sem_inc(xa_ready, 1)
            query(0)
            query(1)
            exps(0, 0)
            for h in range(HALF):
                sums(0, h + 1)
            exps(1, 1)
            rounds(act, body)
            move_xf(T - 1)
            move_xa(T - 2, T % 2)
            for g in range(NG):
                move_turned(T - 1, g)
            move_xa(T - 1, (T - 1) % 2)

        @block.gpsimd
        def _(pool):
            def start(i, u):
                c = slice(u, u + 1)
                pool.wait_ge(e_ready, i * 2 + 2)
                nc.gpsimd.tensor_tensor(goal[:, c], Z1[:, c], Z2[:, c], ALU.add).then_inc(gp, 1)
                pool.wait_ge(gp, 1)
                middle = math.exp(-DEPTH / 2)
                nc.gpsimd.tensor_scalar(mid[:, c], goal[:, c], 0.0, middle, ALU.mult, ALU.add).then_inc(gp, 1)
                nc.gpsimd.tensor_scalar(nmid[:, c], goal[:, c], 0.0, -middle, ALU.mult, ALU.add).then_inc(nmid_ready, 1)
                pool.wait_ge(gp, 2)
                nc.gpsimd.tensor_scalar(goal[:, c], goal[:, c], TOP_P, None, ALU.mult).then_inc(mid_ready, 1)
                pool.sem_clear(gp)

            def move_mid(u, h, sums):
                c = slice(u, u + 1)
                up, down = ratio(h), 1 / ratio(h)
                pool.wait_ge(acc_ready, sums * 2)
                pool.wait_ge(got_ready, sums)
                nc.gpsimd.tensor_tensor(above[:, c], r[:, c], got[:, c], ALU.add).then_inc(gp, 1)
                nc.gpsimd.tensor_scalar(q[:, c], s[:, c], float(S_COLS), mid[:, c], ALU.add, ALU.mult).then_inc(gp, 1)
                pool.wait_ge(gp, 2)
                nc.gpsimd.tensor_scalar(q[:, c], q[:, c], 0.5, above[:, c], ALU.mult, ALU.add).then_inc(gp, 1)
                pool.wait_ge(gp, 3)
                nc.gpsimd.tensor_scalar(q[:, c], q[:, c], goal[:, c], up - down, ALU.is_ge, ALU.mult).then_inc(gp, 1)
                pool.wait_ge(gp, 4)
                nc.gpsimd.tensor_scalar(nmid[:, c], q[:, c], down, nmid[:, c], ALU.add, ALU.mult).then_inc(nmid_ready, 1)
                nc.gpsimd.tensor_scalar(mid[:, c], q[:, c], down, mid[:, c], ALU.add, ALU.mult).then_inc(mid_ready, 1)
                pool.sem_clear(gp)

            def round_(i, u):
                for slot, h, n in halvings(i, u):
                    move_mid(slot, h, first_sum(i) + (n + 1))
                if not fixed(i, 0):
                    xf_sum(i - 1)
                if not beyond(i, T - 2):
                    pool.wait_ge(ends_ready, i * 3 + 3)
                    start(i + 2, u)
                elif fixed(i, T - 2):
                    pool.sem_inc(mid_ready, 1)
                    pool.sem_inc(nmid_ready, 1)

            def xf_sum(i):
                pool.wait_ge(xf_moved, i + 2)
                nc.gpsimd.tensor_tensor(xfs[:, :], xfs[:, :], tile(XF, i), ALU.add).then_inc(xf_chain, 1)
                pool.wait_ge(xf_chain, i + 1)
                nc.gpsimd.tensor_tensor(xfs[:, :], xfs[:, :], cols(m.rdeg, i, 1).broadcast_to([P, D]), ALU.mult) \
                    .then_inc(xf_ready, 1)

            start(0, 0)
            for h in range(HALF):
                move_mid(0, h, h + 1)
            start(1, 1)
            rounds(pool, round_)
            xf_sum(T - 1)

        @block.vector
        def _(dve):
            def rowmax(i, u):
                dve.wait_ge(l_done, i + 2)
                nc.vector.tensor_reduce(mx[:, u:u + 1], lbank, AX.X, ALU.max).then_inc(max_done, 1)
                dve.wait_ge(max_done, i + 1)
                nc.vector.tensor_scalar(nmax[:, u:u + 1], mx[:, u:u + 1], -1.0, None, ALU.mult).then_inc(nmax_ready, 1)

            def summed(u, mids):
                dve.wait_ge(mid_ready, mids)
                nc.vector.scalar_tensor_tensor(masked[:, u, :], E[:, u, 0:V_COLS], mid[:, u:u + 1],
                                               E[:, u, 0:V_COLS], ALU.is_gt, ALU.mult, accum_out=got[:, u:u + 1]) \
                    .then_inc(got_ready, 1)

            PER = 4

            def take_above(i, u, mids):
                end, c = ratio(HALVINGS - 1), slice(u, u + 1)
                dve.wait_ge(mid_ready, mids)
                nc.vector.tensor_scalar(high, mid[:, c], end * (1 + SLACK), None, ALU.mult).then_inc(ends_ready, 1)
                nc.vector.tensor_copy(aim, goal[:, c]).then_inc(ends_ready, 1)
                nc.vector.tensor_scalar(low, mid[:, c], (1 - SLACK) / end, None, ALU.mult).then_inc(ends_ready, 1)
                dve.wait_ge(ends_ready, i * 3 + 3)
                dve.wait_ge(t_done, i * NG + 1)
                nc.vector.scalar_tensor_tensor(A[:, :], E[:, u, :], low, E[:, u, :], ALU.is_gt, ALU.mult,
                                               accum_out=all_).then_inc(s_done, 1)

            def take_interval(i, u):
                dve.wait_ge(s_done, i + 3)
                nc.vector.scalar_tensor_tensor(B[:, :], A[:, :], high, A[:, :], ALU.is_le, ALU.mult,
                                               accum_out=left).then_inc(vec, 1)

            def sum_before(i, u):
                dve.wait_ge(vec, i * PER + 1)
                nc.vector.tensor_tensor(C[:, 0:1], all_, left, ALU.subtract).then_inc(vec, 1)
                dve.wait_ge(vec, i * PER + 2)
                nc.vector.tensor_tensor_scan(C[:, 1:N + 1], B[:, :], B[:, :], C[:, 0:1], ALU.add, ALU.max) \
                    .then_inc(vec, 1)

            def find_cut(i, u):
                dve.wait_ge(vec, i * PER + 3)
                nc.vector.scalar_tensor_tensor(B[:, :], C[:, 0:N], aim, B[:, :], ALU.is_ge, ALU.mult).then_inc(vec, 1)

            def cut(i, u):
                dve.wait_ge(vec, i * PER + 4)
                nc.vector.scalar_tensor_tensor(A[:, :], B[:, :], -1.0, A[:, :], ALU.mult, ALU.add, accum_out=S) \
                    .then_inc(a_ready, 1)

            def invert(i, u):
                dve.wait_ge(a_ready, i + 1)
                if not fixed(i, 0):
                    dve.wait_ge(xa_ready, i)
                nc.vector.reciprocal(rS[:, u:u + 1], S).then_inc(rs_ready, 1)

            steps = (take_interval, sum_before, find_cut, cut, invert)

            def body(i, u):
                for slot, h, n in halvings(i, u):
                    summed(slot, halving_mid(i, n))
                    k = n if fixed(i, T - 1) else n // 2
                    if k < len(steps) and (k == n or n % 2 == 0) and not fixed(i, 0):
                        steps[k](i - 1, 1 - u)
                    if n == 2 * len(steps) and not beyond(i, T - 2):
                        rowmax(i + 2, u)
                take_above(i, u, first_mid(i) + (HALF if fixed(i, T - 1) else 2 * HALF - 1))

            dve.sem_inc(s_done, 2)
            rowmax(0, 0)
            rowmax(1, 1)
            for h in range(HALF):
                summed(0, h + 1)
            rounds(dve, body)
            for step in steps:
                step(T - 1, (T - 1) % 2)


def nucleus_sum(core, m, tag, xa_dram, xf_dram, y_dram, u1_dram, u2_dram, W3, W12, y_out, y_stored):
    nc = core.nc
    sem = lambda n: core.sem(f"{tag}_{n}")
    again = y_out is not None
    XA = core.take(T * D, m.big_b).rearrange("p (t d) -> p t d", t=T)
    XF = core.take(T * D, 0).rearrange("p (t d) -> p t d", t=T)
    KQ = core.take(2 * N).rearrange("p (s n) -> p s n", s=2)
    Y = core.take(T * D, m.ring).rearrange("p (t d) -> p t d", t=T)
    hs = core.take(4 * D).rearrange("p (u d) -> p u d", u=4)
    U = core.take(2 * KD * D, m.big_c).rearrange("p (s k d) -> p s k d", s=2, k=KD)
    hT = core.take(4 * D).rearrange("p (u k n) -> p u k n", u=4, k=KD)
    u_in = sem("weights_loaded")
    x_in, y_in = ([sem(f"{n}_loaded{c}") for c in range(QUARTERS)] for n in "xy")
    TC = T // QUARTERS
    h_ready, t_done, ht_ready, mm_done, y_ready, stored = (sem(n) for n in ("h", "turned", "hT", "products", "y", "stored"))
    with nc.Block() as block:
        @block.sync
        def _(sp):
            sp.dma_start(U[:, 0], u1_dram).then_inc(u_in, 16)
            sp.dma_start(U[:, 1], u2_dram).then_inc(u_in, 16)
            if y_stored is not None:
                sp.wait_ge(y_stored, 16)
            for c in range(QUARTERS):
                part = slice(c * TC, (c + 1) * TC)
                for dst, src, done in ((XF, xf_dram, x_in), (XA, xa_dram, x_in), (Y, y_dram, y_in)):
                    sp.dma_start(dst[:, part, :], src[part, :, :].rearrange("t p d -> p t d")).then_inc(done[c], 16)
            if again:
                with sp.Fori(0, T) as t:
                    sp.wait_ge(y_ready, t + 3)
                    sp.dma_start(rows(y_out, t), tile(Y, t)).then_inc(stored, 16)
                sp.wait_ge(stored, 16 * T)

        @block.scalar
        def _(act):
            for c in range(QUARTERS):
                act.wait_ge(x_in[c], 32)
                with act.Fori(0, TC // 2) as p:
                    t = p * 2 + c * TC
                    for u in range(2):
                        act.wait_ge(t_done, t + (u + 1))
                        nc.scalar.activation(hs[:, 2 * u], tile(XF, t + u), ACT.Copy)
                        nc.scalar.activation(hs[:, 2 * u + 1], tile(XA, t + u), ACT.Copy).then_inc(h_ready, 1)

        @block.tensor
        def _(pe):
            pe.wait_ge(u_in, 32)
            pe.sem_inc(t_done, 2)
            pe.sem_inc(mm_done, 2)
            for c in range(QUARTERS):
                with pe.Fori(0, TC // 2) as p:
                    t = p * 2 + c * TC
                    for u in range(2):
                        pe.wait_ge(h_ready, t + (u + 1))
                        pe.wait_ge(ht_ready, t + (u + 1))
                        for s in range(2):
                            for k in range(KD):
                                last = nc.tensor.transpose(core.bank(2 * u + s)[:, k * P:(k + 1) * P],
                                                           hs[:, 2 * u + s, k * P:(k + 1) * P], m.ident[:, :])
                        last.then_inc(t_done, 1)
                    for u in range(2):
                        pe.wait_ge(ht_ready, t + (u + 3))
                        pe.wait_ge(y_ready, t + (u + 1))
                        last = accumulate(nc, core.bank(4 + u), [(hT[:, 2 * u + s, k], U[:, s, k])
                                                                 for s in range(2) for k in range(KD)])
                        if again:
                            for s, w in enumerate((W3, W12)):
                                last = accumulate(nc, core.bank(6 + u)[0:W2N, s * P:(s + 1) * P],
                                                  [(w[:, k], hT[:, 2 * u + 1, k]) for k in range(KD)])
                        last.then_inc(mm_done, 1)

        @block.vector
        def _(dve):
            dve.sem_inc(ht_ready, 2)
            dve.sem_inc(y_ready, 2)
            for c in range(QUARTERS):
                dve.wait_ge(y_in[c], 16)
                with dve.Fori(0, TC // 2) as p:
                    t = p * 2 + c * TC
                    for u in range(2):
                        dve.wait_ge(t_done, t + (u + 3))
                        dve.wait_ge(mm_done, t + (u + 1))
                        nc.vector.tensor_copy(hT[:, 2 * u:2 * u + 2].rearrange("p u k n -> p (u k n)"),
                                              core.bank(2 * u, 2)).then_inc(ht_ready, 1)
                    for u in range(2):
                        dve.wait_ge(mm_done, t + (u + 3))
                        if again:
                            nc.vector.tensor_copy(KQ[0:W2N, :, bass.ds((t + u) * P, P)],
                                                  core.bank(6 + u)[0:W2N, 0:2 * P].rearrange("p (s n) -> p s n", s=2))
                        y = tile(Y, t + u)
                        nc.vector.tensor_tensor(y, core.bank(4 + u), y, ALU.add).then_inc(y_ready, 1)
    return XA, XF, KQ, Y


def nucleus_out(core, m, Y, x_dram, gamma_dram, beta_dram, out_dram):
    nc = core.nc
    sem = lambda n: core.sem(f"no_{n}")
    X = core.take(T * D, m.big_b).rearrange("p (t d) -> p t d", t=T)
    gamma, beta = core.take(D, m.big_c), core.take(D)
    n1 = core.take(2 * D).rearrange("p (u d) -> p u d", u=2)
    loaded, vec, stats, root, ready, stored, scaled, used = (sem(n) for n in (
        "loaded", "v_chain", "variance", "root", "out_ready", "stored", "scaled", "used"))
    with nc.Block() as block:
        @block.sync
        def _(sp):
            for dst, src in ((gamma[:, :], gamma_dram), (beta[:, :], beta_dram),
                             (X[:, :, :], x_dram.rearrange("t p d -> p t d"))):
                sp.dma_start(dst, src).then_inc(loaded, 16)
            with sp.Fori(0, T) as t:
                sp.wait_ge(ready, t + 1)
                sp.dma_start(rows(out_dram, t), tile(X, t)).then_inc(stored, 16)
            sp.wait_ge(stored, 16 * T)

        @block.scalar
        def _(act):
            act.wait_ge(stats, 1)
            nc.scalar.activation(m.std[:, :], m.var[:, :], ACT.Sqrt).then_inc(root, 1)

        @block.gpsimd
        def _(pool):
            pool.wait_ge(loaded, 48)
            with pool.Fori(0, T) as t:
                nc.gpsimd.tensor_tensor(tile(X, t), tile(X, t), beta[:, :], ALU.add).then_inc(used, 1)

        @block.vector
        def _(dve):
            link = Chain(dve, vec)
            for t in range(T):
                link(nc.vector.bn_stats(m.st[:, :], Y[:, t]))
                link(nc.vector.bn_aggr(m.mv[:, t], m.st[:, :]))
            nc.vector.tensor_scalar_add(m.var[:, :], m.mv[:, :, 1], LN_EPS).then_inc(stats, 1)
            dve.wait_ge(root, 1)
            link(nc.vector.reciprocal(m.rstd[:, :], m.std[:, :]))
            dve.wait_ge(loaded, 48)
            with dve.Fori(0, T) as t:
                step = Chain(dve, vec, t * 2 + link.k)
                mean = m.mv[:, bass.ds(t, 1), 0:1].rearrange("p a b -> p (a b)")
                step(nc.vector.tensor_scalar(n1[:, 0], tile(Y, t), mean, cols(m.rstd, t, 1), ALU.subtract, ALU.mult))
                step(nc.vector.tensor_tensor(n1[:, 1], n1[:, 0], gamma[:, :], ALU.mult))
                dve.wait_ge(used, t + 1)
                nc.vector.tensor_tensor(tile(X, t), tile(X, t), n1[:, 1], ALU.add).then_inc(ready, 1)


def dot_attention(core, m, x_dram, adj_dram, weights, biases, x_out):
    nc = core.nc
    sem = lambda n: core.sem(f"dot_{n}")
    W = [core.take(KD * D, n * KD * D).rearrange("p (k d) -> p k d", k=KD) for n in range(3)]
    kT = core.take(T * D, T * D).rearrange("p (k n) -> p k n", k=KD)
    qT = core.take(T * D, m.big_b).rearrange("p (k n) -> p k n", k=KD)
    V = core.take(T * D, m.big_c).rearrange("p (t d) -> p t d", t=T)
    bv, bq, bk = core.take(D, m.w), core.take(KD), core.take(KD)

    def project(nc, hT, u):
        for n in range(2):
            for c in range(KD):
                accumulate(nc, core.bank(2 + u + 2 * n)[:, c * P:(c + 1) * P],
                           [(W[n][:, k, c * P:(c + 1) * P], hT[:, k]) for k in range(KD)])
        return accumulate(nc, core.bank(6 + u), [(hT[:, k], W[2][:, k]) for k in range(KD)])

    def evac_dve(nc, t, u):
        for n, (dst, bias) in enumerate(((qT, bq), (kT, bk))):
            nc.vector.tensor_tensor(dst[:, :, bass.ds(t * P, P)], core.bank(2 + u + 2 * n).rearrange("p (k n) -> p k n", k=KD),
                                    bias.unsqueeze(2).broadcast_to([P, KD, P]), ALU.add)
        return nc.vector.tensor_tensor(tile(V, t), core.bank(6 + u), bv[:, :], ALU.add)

    front(core, m, "dot", x_dram, [(w[:, :, :], d) for w, d in zip(W, weights)]
          + [(bq[:, :], biases[0]), (bk[:, :], biases[1]), (bv[:, :], biases[2])], project=project, evac_dve=evac_dve)

    adj = core.take(2 * N, m.ring).rearrange("p (u n) -> p u n", u=2)
    s, b, A = core.take(N), core.take(N), core.take(N)
    AT = core.take(N).rearrange("p (t n) -> p t n", t=T)
    qs = core.take(D, 0).rearrange("p (k n) -> p k n", k=KD)
    xt = core.take(2 * D).rearrange("p (u d) -> p u d", u=2)
    o = core.take(D)
    small = core.take(8)
    mx, nmax, Z, rZ = (small[:, n:n + 1] for n in range(4))
    G, NG = 4, T // 4
    SCALE = 1.0 / float(D) ** 0.5
    lbank, mbank = core.bank(0, 4), core.bank(6)
    adj_in, x_in = [sem(f"adj{u}") for u in range(2)], [sem(f"x{u}") for u in range(2)]
    q_ready, l_done, l_read, max_ready, e_ready, t_done, t_moved, m_done, o_ready, stored, vec, r_ready = (
        sem(n) for n in ("q", "logits", "logits_read", "max", "exp", "turned", "turned_moved", "product", "out",
                         "stored", "v_chain", "reciprocal"))

    with nc.Block() as block:
        @block.sync
        def _(sp):
            def load(i, u):
                sp.wait_ge(o_ready, i + 1)
                sp.dma_start(adj[:, u], rows(adj_dram, i)).then_inc(adj_in[u], 16)
                sp.dma_start(xt[:, u], rows(x_dram, i)).then_inc(x_in[u], 16)

            def store(i, u):
                sp.wait_ge(o_ready, i + 3)
                sp.dma_start(rows(x_out, i), xt[:, u]).then_inc(stored, 16)
                sp.wait_ge(stored, i * 16 + 16)

            load(0, 0)
            load(1, 1)
            with sp.Fori(0, T // 2 - 1) as p:
                for u in range(2):
                    store(p * 2 + u, u)
                    load(p * 2 + (u + 2), u)
            store(T - 2, 0)
            store(T - 1, 1)

        @block.tensor
        def _(pe):
            def logits(i, u):
                pe.wait_ge(q_ready, i + 1)
                pe.wait_ge(l_read, i + 1)
                for c in range(N // BANK):
                    last = accumulate(nc, core.bank(c), [(qs[:, k], kT[:, k, c * BANK:(c + 1) * BANK]) for k in range(KD)])
                last.then_inc(l_done, 1)

            def product(i, u):
                pe.wait_ge(e_ready, i + 1)
                for g in range(NG):
                    pe.wait_ge(t_moved, i * NG + (g + 1))
                    for c in range(G):
                        last = nc.tensor.transpose(core.bank(4 + g % 2)[:, c * P:(c + 1) * P],
                                                   A[:, (g * G + c) * P:(g * G + c + 1) * P], m.ident[:, :])
                    last.then_inc(t_done, 1)
                pe.wait_ge(t_moved, i * NG + (NG + 2))
                pe.wait_ge(o_ready, i + 2)
                accumulate(nc, mbank, [(AT[:, jt], V[:, jt]) for jt in range(T)]).then_inc(m_done, 1)

            pe.sem_inc(l_done, 1)
            pe.sem_inc(m_done, 1)
            pe.sem_inc(t_done, 1)
            tiles_ahead(pe, logits, product)

        @block.scalar
        def _(act):
            def query(i):
                act.wait_ge(l_done, i + 1)
                nc.scalar.activation(qs[:, :, :], qT[:, :, bass.ds(i * P, P)], ACT.Copy).then_inc(q_ready, 1)

            def exps(i, u):
                if not (type(i) is int and i == T - 1):
                    query(i + 1)
                act.wait_ge(max_ready, i + 1)
                act.wait_ge(t_done, i * NG + 1)
                act.wait_ge(r_ready, i + 1)
                nc.scalar.activation(A[:, :], s[:, :], ACT.Exp, bias=nmax, accum_out=Z).then_inc(e_ready, 1)

            def moves(i, u):
                act.wait_ge(m_done, i + 1)
                for g in range(NG):
                    act.wait_ge(t_done, i * NG + (g + 2))
                    nc.scalar.activation(AT[:, g * G:(g + 1) * G, :],
                                         core.bank(4 + g % 2).rearrange("p (c n) -> p c n", c=G), ACT.Copy) \
                        .then_inc(t_moved, 1)

            act.sem_inc(t_moved, 2)
            query(0)
            exps(0, 0)
            with act.Fori(0, T - 2) as i:
                moves(i, 0)
                exps(i + 1, 0)
            moves(T - 2, 0)
            exps(T - 1, 0)
            moves(T - 1, 0)

        @block.vector
        def _(dve):
            PER = 4

            def mask(i, u):
                link = Chain(dve, vec, i * PER)
                dve.wait_ge(l_done, i + 2)
                dve.wait_ge(e_ready, i) if not (type(i) is int and i == 0) else None
                dve.wait_ge(adj_in[u], (i - u) * 8 + 16)
                nc.vector.scalar_tensor_tensor(s[:, :], lbank, SCALE, adj[:, u], ALU.mult, ALU.mult).then_inc(l_read, 1)
                dve.wait_ge(l_read, i + 2)
                link(nc.vector.tensor_scalar(b[:, :], s[:, :], 0.0, NOTHING, ALU.is_equal, ALU.mult))
                link(nc.vector.tensor_tensor(s[:, :], s[:, :], b[:, :], ALU.add))
                link(nc.vector.tensor_reduce(mx, s[:, :], AX.X, ALU.max))
                link(nc.vector.tensor_scalar(nmax, mx, -1.0, None, ALU.mult))
                dve.sem_inc(max_ready, 1)

            def out(i, u):
                dve.wait_ge(e_ready, i + 1)
                nc.vector.reciprocal(rZ, Z).then_inc(r_ready, 1)
                dve.wait_ge(r_ready, i + 2)
                dve.wait_ge(m_done, i + 2)
                nc.vector.tensor_scalar(o[:, :], mbank, rZ, 0.0, ALU.mult, ALU.max).then_inc(o_chain, 1)
                dve.wait_ge(o_chain, i + 1)
                dve.wait_ge(x_in[u], (i - u) * 8 + 16)
                nc.vector.tensor_tensor(xt[:, u], xt[:, u], o[:, :], ALU.add).then_inc(o_ready, 1)

            o_chain = sem("o_chain")
            dve.sem_inc(l_read, 1)
            dve.sem_inc(r_ready, 1)
            dve.sem_inc(o_ready, 2)
            mask(0, 0)
            with dve.Fori(0, T // 2 - 1) as p:
                mask(p * 2 + 1, 1)
                out(p * 2, 0)
                mask(p * 2 + 2, 0)
                out(p * 2 + 1, 1)
            mask(T - 1, 1)
            out(T - 2, 0)
            out(T - 1, 1)


def mlp_out(core, m, hid, x_dram, w, b, out_dram):
    nc = core.nc
    sem = lambda n: core.sem(f"mlp_{n}")
    X = core.take(T * D, m.ring).rearrange("p (t d) -> p t d", t=T)
    hs = core.take(2 * D).rearrange("p (u d) -> p u d", u=2)
    hT = core.take(2 * D).rearrange("p (u k n) -> p u k n", u=2, k=KD)
    D1, D2, D3 = D // 2, D // 4, D // 2
    W1 = core.take(KD * D1, m.w).rearrange("p (k d) -> p k d", k=KD)
    W2 = core.take(D1 // P * D2).rearrange("p (k d) -> p k d", k=D1 // P)
    W3 = core.take(D2 // P * D3).rearrange("p (k d) -> p k d", k=D2 // P)
    W4 = core.take(D3 // P * D).rearrange("p (k d) -> p k d", k=D3 // P)
    b4 = core.take(D)
    b1, b2, b3 = core.take(D1 // P), core.take(D2 // P), core.take(D3 // P)
    lo, ex, up = (core.take(2 * D, m.big_c + 2 * D * n).rearrange("p (u d) -> p u d", u=2) for n in range(3))
    o1 = core.take(2 * D1).rearrange("p (u k n) -> p u k n", u=2, k=D1 // P)
    o2 = core.take(2 * D2).rearrange("p (u k n) -> p u k n", u=2, k=D2 // P)
    o3 = core.take(2 * D3).rearrange("p (u k n) -> p u k n", u=2, k=D3 // P)
    w_in, x_in = sem("weights_loaded"), sem("x_loaded")
    lo_ready, ex_ready, h_ready, t_done, ht_ready, o_ready, stored, vec = (sem(n) for n in (
        "lo", "exp", "h", "turned", "hT", "out", "stored", "v_chain"))
    mm = [sem(f"product{n}") for n in range(4)]
    moved = [sem(f"layer{n}") for n in range(3)]
    biased = sem("biased")
    with nc.Block() as block:
        @block.sync
        def _(sp):
            for dst, src in [(W1, w[0]), (W2, w[1]), (W3, w[2]), (W4, w[3])]:
                sp.dma_start(dst[:, :, :], src).then_inc(w_in, 16)
            for dst, src in [(b1, b[0]), (b2, b[1]), (b3, b[2]), (b4, b[3])]:
                sp.dma_start(dst[:, :], src).then_inc(w_in, 16)
            sp.dma_start(X[:, :, :], x_dram.rearrange("t p d -> p t d")).then_inc(x_in, 16)
            with sp.Fori(0, T) as t:
                sp.wait_ge(o_ready, t + 3)
                sp.dma_start(rows(out_dram, t), tile(X, t)).then_inc(stored, 16)
            sp.wait_ge(stored, 16 * T)

        @block.vector
        def _(dve):
            dve.sem_inc(ht_ready, 2)
            dve.sem_inc(h_ready, 2)
            dve.sem_inc(o_ready, 2)

            def elu(t):
                for u in range(2):
                    dve.wait_ge(ex_ready, t + (u + 1))
                    nc.vector.tensor_scalar_min(lo[:, u], tile(hid, t + u), 0.0).then_inc(lo_ready, 1)
                for u in range(2):
                    dve.wait_ge(ex_ready, t + (u + 3))
                    dve.wait_ge(t_done, t + (u + 1))
                    nc.vector.scalar_tensor_tensor(up[:, u], tile(hid, t + u), 0.0, ex[:, u], ALU.max, ALU.add) \
                        .then_inc(vec, 1)
                    dve.wait_ge(vec, t + (u + 1))
                    nc.vector.tensor_scalar(hs[:, u], up[:, u], -1.0, None, ALU.add).then_inc(h_ready, 1)

            def move(t):
                for u in range(2):
                    dve.wait_ge(t_done, t + (u + 3))
                    dve.wait_ge(mm[0], t + (u + 1))
                    nc.vector.tensor_copy(hT[:, u], core.bank(u).rearrange("p (k n) -> p k n", k=KD)) \
                        .then_inc(ht_ready, 1)

            def out(t):
                for u in range(2):
                    x = tile(X, t + u)
                    nc.vector.tensor_tensor(x, x, b4[:, :], ALU.add).then_inc(biased, 1)
                    dve.wait_ge(biased, t + (u + 1))
                    dve.wait_ge(mm[3], t + (u + 3))
                    nc.vector.tensor_tensor(x, core.bank(6 + u), x, ALU.add).then_inc(o_ready, 1)

            elu(0)
            dve.wait_ge(w_in, 16 * 8)
            dve.wait_ge(x_in, 16)
            with dve.Fori(0, T // 2 - 1) as p:
                move(p * 2)
                elu(p * 2 + 2)
                out(p * 2)
            move(T - 2)
            out(T - 2)

        @block.scalar
        def _(act):
            act.sem_inc(ex_ready, 2)
            for n in range(3):
                act.sem_inc(moved[n], 2)

            def exps(t):
                for u in range(2):
                    act.wait_ge(lo_ready, t + (u + 1))
                    act.wait_ge(h_ready, t + (u + 1))
                    nc.scalar.activation(ex[:, u], lo[:, u], ACT.Exp).then_inc(ex_ready, 1)

            def move(n, o, bias, t):
                for u in range(2):
                    act.wait_ge(mm[n], t + (u + 3))
                    act.wait_ge(mm[n + 1], t + (u + 1))
                    for c in range(o.shape[2]):
                        last = nc.scalar.activation(o[:, u, c], core.bank(2 + u + (2 if n == 1 else 0))[:, c * P:(c + 1) * P],
                                                    ACT.Relu, bias=bias[:, c:c + 1])
                    last.then_inc(moved[n], 1)

            exps(0)
            act.wait_ge(w_in, 16 * 8)
            with act.Fori(0, T // 2 - 1) as p:
                exps(p * 2 + 2)
                for n, (o, bias) in enumerate(((o1, b1), (o2, b2), (o3, b3))):
                    move(n, o, bias, p * 2)
            for n, (o, bias) in enumerate(((o1, b1), (o2, b2), (o3, b3))):
                move(n, o, bias, T - 2)

        @block.tensor
        def _(pe):
            pe.sem_inc(t_done, 2)
            for n in range(4):
                pe.sem_inc(mm[n], 2)
            pe.wait_ge(w_in, 16 * 8)
            with pe.Fori(0, T // 2) as p:
                for u in range(2):
                    pe.wait_ge(h_ready, p * 2 + (u + 3))
                    pe.wait_ge(ht_ready, p * 2 + (u + 1))
                    for k in range(KD):
                        last = nc.tensor.transpose(core.bank(u)[:, k * P:(k + 1) * P],
                                                   hs[:, u, k * P:(k + 1) * P], m.ident[:, :])
                    last.then_inc(t_done, 1)
                for u in range(2):
                    pe.wait_ge(ht_ready, p * 2 + (u + 3))
                    pe.wait_ge(moved[2], p * 2 + (u + 1))
                    for c in range(D1 // P):
                        last = accumulate(nc, core.bank(2 + u)[:, c * P:(c + 1) * P],
                                          [(W1[:, k, c * P:(c + 1) * P], hT[:, u, k]) for k in range(KD)])
                    last.then_inc(mm[0], 1)
                for u in range(2):
                    pe.wait_ge(moved[0], p * 2 + (u + 3))
                    accumulate(nc, core.bank(4 + u)[:, 0:P], [(W2[:, k], o1[:, u, k]) for k in range(D1 // P)]) \
                        .then_inc(mm[1], 1)
                for u in range(2):
                    pe.wait_ge(moved[1], p * 2 + (u + 3))
                    for c in range(D3 // P):
                        last = accumulate(nc, core.bank(2 + u)[:, c * P:(c + 1) * P],
                                          [(W3[:, k, c * P:(c + 1) * P], o2[:, u, k]) for k in range(D2 // P)])
                    last.then_inc(mm[2], 1)
                for u in range(2):
                    pe.wait_ge(moved[2], p * 2 + (u + 3))
                    pe.wait_ge(o_ready, p * 2 + (u + 1))
                    accumulate(nc, core.bank(6 + u), [(o3[:, u, k], W4[:, k]) for k in range(D3 // P)]).then_inc(mm[3], 1)


def graph_layers_kernel(nc, io):
    with ExitStack() as ctx:
        core = Core(nc, ctx)
        m = layout(core)
        m.adj_loaded, m.adj_loads = ctx.enter_context(nc.semaphore("adjacency_loaded")), 0
        dram = lambda name, shape=(T, P, D): nc.dram_tensor(name, list(shape), F32, kind="Internal").ap()
        x1, x2, x3 = dram("x1"), dram("x2"), dram("x3")
        y0, y1, xa1, xf1, xa2, xf2 = (dram(n) for n in ("y0", "y1", "xa1", "xf1", "xa2", "xf2"))
        tiles = lambda a: a.rearrange("(t p) d -> t p d", p=P)
        chunks = lambda a: a.rearrange("(k p) d -> p k d", p=P)
        adj, adjT = tiles(io["adj"]), tiles(io["adjT"])
        with core.layer():
            setup(core, m)
            hid = graph_attention(core, m, "gat0", 16, tiles(io["x"]), adjT, chunks(io["L0_W"]),
                                  io["L0_a1"], io["L0_a2"], dram("c0", (16, N)), True)
            mix_out(core, m, "mix0", hid, tiles(io["x"]), chunks(io["L0_W_out"]), io["L0_b_out"], x1)
        with core.layer():
            XA, KQ, W3, W12, y0_stored = nucleus_front(core, m, x1, io["L1_W1T"], io["L1_W2"], chunks(io["L1_W3"]), y0)
            nucleus_step(core, m, "n0", XA, XA, KQ, adjT, xa1, xf1)
            XA, XF, KQ, _ = nucleus_sum(core, m, "s0", xa1, xf1, y0, chunks(io["L1_U1_0"]), chunks(io["L1_U2_0"]),
                                        W3, W12, y1, y0_stored)
            nucleus_step(core, m, "n1", XA, XF, KQ, adjT, xa2, xf2)
            _, _, _, Y = nucleus_sum(core, m, "s1", xa2, xf2, y1, chunks(io["L1_U1_1"]), chunks(io["L1_U2_1"]),
                                     W3, W12, None, None)
            nucleus_out(core, m, Y, x1, io["L1_gamma"], io["L1_beta"], x2)
        with core.layer():
            dot_attention(core, m, x2, adj, [chunks(io[f"L2_W{n}T"]) for n in "qkv"], [io[f"L2_b{n}"] for n in "qkv"], x3)
        with core.layer():
            hid = graph_attention(core, m, "gat3", 8, x3, adjT, chunks(io["L3_W"]), io["L3_a1"], io["L3_a2"],
                                  dram("c3", (8, N)), False)
            mlp_out(core, m, hid, x3, [chunks(io[f"L3_W{n}T"]) for n in range(1, 5)],
                    [io[f"L3_b{n}"] for n in range(1, 5)], tiles(io["out"]))


def kernel(**inputs):
    import numpy as np
    import concourse.bacc as bacc
    from concourse.bass_utils import run_bass_kernel_spmd

    a = {k: np.asarray(v) for k, v in inputs.items()}
    wide = lambda v: np.ascontiguousarray(np.broadcast_to(v.reshape(1, -1), (P, v.size)))
    column = lambda v: np.ascontiguousarray(v.reshape(-1, P).T)
    arrays = {
        "x": a["x"], "adj": a["adj"], "adjT": a["adj"].T,
        "L0_W": a["L0_gnn_W_seq"], "L0_a1": wide(np.tile(a["L0_gnn_a1"], 16)), "L0_a2": wide(np.tile(a["L0_gnn_a2"], 16)),
        "L0_W_out": a["L0_gnn_W_out"], "L0_b_out": wide(a["L0_gnn_b_out"]),
        "L1_W1T": a["L1_gnn_W1"].T, "L1_W2": a["L1_gnn_W2"], "L1_W3": a["L1_gnn_W3"],
        **{f"L1_U{n}": a[f"L1_gnn_U{n}"] for n in ("1_0", "1_1", "2_0", "2_1")},
        "L1_gamma": wide(a["L1_gnn_gamma"]), "L1_beta": wide(a["L1_gnn_beta"]),
        **{f"L2_W{n}T": a[f"L2_gnn_W_{n}"].T for n in "qkv"},
        "L2_bq": column(a["L2_gnn_b_q"]), "L2_bk": column(a["L2_gnn_b_k"]), "L2_bv": wide(a["L2_gnn_b_v"]),
        "L3_W": a["L3_gnn_W"].transpose(1, 0, 2).reshape(D, D),
        "L3_a1": wide(a["L3_gnn_a1"]), "L3_a2": wide(a["L3_gnn_a2"]),
        **{f"L3_W{n}T": a[f"L3_gnn_W{n}"].T for n in range(1, 5)},
        **{f"L3_b{n}": column(a[f"L3_gnn_b{n}"]) for n in range(1, 4)}, "L3_b4": wide(a["L3_gnn_b4"]),
    }
    nc = bacc.Bacc("TRN2", target_bir_lowering=False, num_devices=1)
    io = {}
    for name, v in arrays.items():
        arrays[name] = v = np.ascontiguousarray(v)
        io[name] = nc.dram_tensor(name, v.shape, mybir.dt.from_np(v.dtype), kind="ExternalInput").ap()
    io["out"] = nc.dram_tensor("out", (N, D), F32, kind="ExternalOutput").ap()
    graph_layers_kernel(nc, io)
    r = run_bass_kernel_spmd(nc, [arrays], core_ids=[0])
    return r.results[0]["out"]
```
